# Optimizing a Trainium2 kernel written in Bass

```python
import numpy as np
import jax
import jax.numpy as jnp

def _softmax(x, axis=-1):
    return jax.nn.softmax(x, axis=axis)

def _gelu(x):
    return jax.nn.gelu(x, approximate=True)

def _silu(x):
    return jax.nn.silu(x)

def _sigmoid(x):
    return jax.nn.sigmoid(x)

def _layernorm(x, axis=-1, eps=1e-05):
    m = jnp.mean(x, axis=axis, keepdims=True)
    v = jnp.var(x, axis=axis, keepdims=True)
    return (x - m) / jnp.sqrt(v + eps)

def _scatter_add(tgt, idx, src, axis=0):
    return tgt.at[idx].add(src)

def _segment_sum(src, seg, n):
    return jax.ops.segment_sum(src, seg, n)
kernel_name = 'mk_vit_tower_d1_tok_img1024_r4_b8f14a'

def setup_inputs(seed: int=0):
    np.random.seed(seed)
    _w = jnp.asarray

    def _rec_inputs():
        import jax
        import jax.numpy as jnp
        _rk = jax.random.key(seed)
        x = -0.000222058 + 0.999998 * jax.random.normal(jax.random.fold_in(_rk, 1), (64, 3, 64, 64), jnp.float32)
        return x
    x = _rec_inputs()

    def _L0_tok_setup():
        import jax, jax.numpy as jnp
        import numpy as np
        IMG, PS, C, OUT = (64, 16, 3, 256)
        NP = IMG // PS
        IN_FEAT = C * PS * PS
        key = jax.random.key(seed)
        k1, k2, k3, k4 = jax.random.split(key, 4)
        x = jax.random.normal(k1, (128, C, IMG, IMG), dtype=jnp.float32)
        W = jax.random.normal(k2, (OUT, IN_FEAT), dtype=jnp.float32) / np.sqrt(IN_FEAT)
        b = jax.random.normal(k3, (OUT,), dtype=jnp.float32) * 0.01
        pos_emb = jax.random.normal(k4, (NP * NP, OUT), dtype=jnp.float32)
        return {'x': x, 'W': W, 'b': b, 'pos_emb': pos_emb}
    _L0_tok_all = _L0_tok_setup()
    _L0_tok_in = {k: v for k, v in _L0_tok_all.items() if k in ('W', 'b', 'pos_emb')}
    del _L0_tok_all

    def _L0_attn_setup():
        import jax, jax.numpy as jnp
        import numpy as np
        B, T, D = (2, 512, 256)
        H = 16
        HD = D // H
        DL = 128
        NR = 64
        EPS = 1.1920929e-07

        def _rms_norm(x, w):
            ms = jnp.mean(jnp.square(x), axis=-1, keepdims=True)
            return x * jax.lax.rsqrt(ms + EPS) * w
        key = jax.random.key(seed)
        ks = jax.random.split(key, 10)
        s = 0.02
        return {'x': jax.random.normal(ks[0], (B, T, D), dtype=jnp.float32), 'W_DQ': jax.random.normal(ks[1], (DL, HD), dtype=jnp.float32) * s, 'W_UQ': jax.random.normal(ks[2], (HD, DL), dtype=jnp.float32) * s, 'W_DKV': jax.random.normal(ks[3], (2 * DL, HD), dtype=jnp.float32) * s, 'W_UKV': jax.random.normal(ks[4], (2 * HD, 2 * DL), dtype=jnp.float32) * s, 'W_QR': jax.random.normal(ks[5], (NR, HD), dtype=jnp.float32) * s, 'W_KR': jax.random.normal(ks[6], (NR, HD), dtype=jnp.float32) * s, 'W_O': jax.random.normal(ks[7], (HD, HD), dtype=jnp.float32) * s, 'q_norm_w': jnp.ones((HD,), dtype=jnp.float32), 'k_norm_w': jnp.ones((HD,), dtype=jnp.float32)}
    _L0_attn_all = _L0_attn_setup()
    _L0_attn_in = {k: v for k, v in _L0_attn_all.items() if k in ('W_DQ', 'W_UQ', 'W_DKV', 'W_UKV', 'W_QR', 'W_KR', 'W_O', 'q_norm_w', 'k_norm_w')}
    del _L0_attn_all

    def _L0_ffn_setup():
        import jax, jax.numpy as jnp
        import numpy as np
        B, S, D, F, E = (4, 512, 256, 1024, 4)
        key = jax.random.key(seed)
        ks = jax.random.split(key, 8)
        sd = 1.0 / np.sqrt(D)
        sf = 1.0 / np.sqrt(F)
        return {'x': jax.random.normal(ks[0], (B, S, D), dtype=jnp.float32), 'W1': jax.random.uniform(ks[1], (E, D, F), jnp.float32, -sd, sd), 'b1': jax.random.uniform(ks[2], (E, F), jnp.float32, -sd, sd), 'W2': jax.random.uniform(ks[3], (E, F, D), jnp.float32, -sf, sf), 'b2': jax.random.uniform(ks[4], (E, D), jnp.float32, -sf, sf), 'Wu': jax.random.uniform(ks[5], (D, 1), jnp.float32, -sd, sd), 'bu': jax.random.uniform(ks[6], (1,), jnp.float32, -sd, sd)}
    _L0_ffn_all = _L0_ffn_setup()
    _L0_ffn_in = {k: v for k, v in _L0_ffn_all.items() if k in ('W1', 'b1', 'W2', 'b2', 'Wu', 'bu')}
    del _L0_ffn_all
    return {'x': x, 'L0_tok_W': _L0_tok_in['W'], 'L0_tok_b': _L0_tok_in['b'], 'L0_tok_pos_emb': _L0_tok_in['pos_emb'], 'L0_attn_W_DQ': _L0_attn_in['W_DQ'], 'L0_attn_W_UQ': _L0_attn_in['W_UQ'], 'L0_attn_W_DKV': _L0_attn_in['W_DKV'], 'L0_attn_W_UKV': _L0_attn_in['W_UKV'], 'L0_attn_W_QR': _L0_attn_in['W_QR'], 'L0_attn_W_KR': _L0_attn_in['W_KR'], 'L0_attn_W_O': _L0_attn_in['W_O'], 'L0_attn_q_norm_w': _L0_attn_in['q_norm_w'], 'L0_attn_k_norm_w': _L0_attn_in['k_norm_w'], 'L0_ffn_W1': _L0_ffn_in['W1'], 'L0_ffn_b1': _L0_ffn_in['b1'], 'L0_ffn_W2': _L0_ffn_in['W2'], 'L0_ffn_b2': _L0_ffn_in['b2'], 'L0_ffn_Wu': _L0_ffn_in['Wu'], 'L0_ffn_bu': _L0_ffn_in['bu']}

def reference(x, L0_tok_W, L0_tok_b, L0_tok_pos_emb, L0_attn_W_DQ, L0_attn_W_UQ, L0_attn_W_DKV, L0_attn_W_UKV, L0_attn_W_QR, L0_attn_W_KR, L0_attn_W_O, L0_attn_q_norm_w, L0_attn_k_norm_w, L0_ffn_W1, L0_ffn_b1, L0_ffn_W2, L0_ffn_b2, L0_ffn_Wu, L0_ffn_bu):
    import jax
    import jax.numpy as jnp

    def _L0_tok_ref(x, W, b, pos_emb):
        import jax, jax.numpy as jnp
        import numpy as np
        IMG, PS, C, OUT = (64, 16, 3, 256)
        NP = IMG // PS
        IN_FEAT = C * PS * PS
        B = x.shape[0]
        p = x.reshape(B, C, NP, PS, NP, PS).transpose(0, 1, 2, 4, 3, 5)
        p = p.transpose(0, 2, 3, 1, 4, 5)
        p = p.reshape(B, NP * NP, IN_FEAT)
        out = jnp.einsum('bnf,of->bno', p, W) + b + pos_emb
        return out

    def _L0_attn_ref(x, W_DQ, W_UQ, W_DKV, W_UKV, W_QR, W_KR, W_O, q_norm_w, k_norm_w):
        import jax, jax.numpy as jnp
        import numpy as np
        B, T, D = (2, 512, 256)
        H = 16
        HD = D // H
        DL = 128
        NR = 64
        EPS = 1.1920929e-07

        def _rms_norm(x, w):
            ms = jnp.mean(jnp.square(x), axis=-1, keepdims=True)
            return x * jax.lax.rsqrt(ms + EPS) * w
        b, t, d = x.shape
        scale = HD ** (-0.5)
        xh = x.reshape(b, t, H, HD).transpose(0, 2, 1, 3)
        c_q = jnp.einsum('bhtd,ld->bhtl', xh, W_DQ)
        q_c = jnp.einsum('bhtl,dl->bhtd', c_q, W_UQ)
        q_c_norm = _rms_norm(q_c, q_norm_w)
        q_r = jnp.einsum('bhtd,rd->bhtr', q_c_norm, W_QR)
        q = jnp.concatenate([q_c_norm, q_r], axis=-1)
        c_kv = jnp.einsum('bhtd,ld->bhtl', xh, W_DKV)
        kv = jnp.einsum('bhtl,dl->bhtd', c_kv, W_UKV)
        k_c, v_c = (kv[..., :HD], kv[..., HD:])
        k_c_norm = _rms_norm(k_c, k_norm_w)
        k_r = jnp.einsum('bhtd,rd->bhtr', xh, W_KR)
        k = jnp.concatenate([k_c_norm, k_r], axis=-1)
        scores = jnp.einsum('bhqd,bhkd->bhqk', q, k) * scale
        causal = jnp.triu(jnp.full((t, t), -jnp.inf, dtype=scores.dtype), k=1)
        attn = jax.nn.softmax(scores + causal, axis=-1)
        ctx = jnp.einsum('bhqk,bhkd->bhqd', attn, v_c)
        out = jnp.einsum('bhtd,od->bhto', ctx, W_O)
        return out.transpose(0, 2, 1, 3).reshape(b, t, d)

    def _L0_ffn_ref(x, W1, b1, W2, b2, Wu, bu):
        import jax, jax.numpy as jnp
        import numpy as np
        B, S, D, F, E = (4, 512, 256, 1024, 4)
        n_exp = W1.shape[0]
        seq = x.shape[1]
        u = jax.nn.sigmoid(jnp.einsum('bsd,do->bso', x, Wu) + bu)[..., 0]
        k = jnp.clip(jnp.ceil(u * n_exp), 1, n_exp).astype(jnp.int32)
        h = jax.nn.relu(jnp.einsum('bsd,edf->bsef', x, W1) + b1)
        y = jnp.einsum('bsef,efd->bsed', h, W2) + b2
        s_idx = jnp.arange(seq)
        out = jnp.zeros_like(x)
        for i in range(1, n_exp + 1):
            e_idx = (s_idx + i - 1) % n_exp
            y_i = jnp.take_along_axis(y, e_idx[None, :, None, None], axis=2)[:, :, 0, :]
            w = jnp.where(k >= i, u / i, 0.0)
            out = out + w[..., None] * y_i
        return out
    h = _L0_tok_ref(x, L0_tok_W, L0_tok_b, L0_tok_pos_emb)
    h = h + _L0_attn_ref(_layernorm(h, axis=-1), L0_attn_W_DQ, L0_attn_W_UQ, L0_attn_W_DKV, L0_attn_W_UKV, L0_attn_W_QR, L0_attn_W_KR, L0_attn_W_O, L0_attn_q_norm_w, L0_attn_k_norm_w)
    h = h + _L0_ffn_ref(_layernorm(h, axis=-1), L0_ffn_W1, L0_ffn_b1, L0_ffn_W2, L0_ffn_b2, L0_ffn_Wu, L0_ffn_bu)
    return h

_drawn_inputs = setup_inputs


def setup_inputs(seed=0):
    import zlib

    import numpy as np

    out = dict(_drawn_inputs(seed))
    spreads = {'L0_attn_q_norm_w': (1.0, 0.6), 'L0_attn_k_norm_w': (1.0, 0.6)}
    factors = {'L0_tok_b': 7.655,
     'L0_attn_W_DQ': 8.0,
     'L0_attn_W_UQ': 8.0,
     'L0_attn_W_DKV': 8.0,
     'L0_attn_W_UKV': 8.0,
     'L0_attn_W_QR': 8.0,
     'L0_attn_W_KR': 8.0,
     'L0_attn_W_O': 8.0,
     'L0_ffn_b1': 8.0,
     'L0_ffn_b2': 7.837}
    for name, (base, spread) in spreads.items():
        noise = np.random.default_rng([zlib.crc32(name.encode()), seed]).standard_normal(out[name].shape)
        drawn = base * np.exp(spread * noise) if base else spread * noise
        out[name] = jnp.asarray(drawn.astype(out[name].dtype))
    for name, factor in factors.items():
        out[name] = (out[name] * factor).astype(out[name].dtype)
    return out
```

```python
from contextlib import ExitStack

import numpy as np
import concourse.bass as bass
from concourse import mybir

F32 = mybir.dt.float32
F32R = mybir.dt.float32r
ALU = mybir.AluOpType
ACT = mybir.ActivationFunctionType
AXX = mybir.AxisListType.X

P = 128
D = 256
NC_ = D // P
H, HD = 16, 16
HC = P // HD
T = 16
IMGS = 64
TOK = IMGS * T
GROUPS = TOK // P
GI = P // T
HALF_GROUPS = GROUPS // 2
HT = TOK // 2
KF = 768 // P
E = 4
FF = 1024
FC = FF // P
CLS = 4
LN_EPS = 1e-5
RMS_EPS = 1.1920929e-07
SCALE = HD ** -0.5
MASKED = -1e30
LN3 = float(np.log(3.0))
THRESH = [None, -LN3, 0.0, LN3]
XR = 3
UNITS = [(0, 0), (1, 0), (0, 1), (1, 1), (2, 0), (2, 1), (3, 0), (3, 1)]
STAGES = 8
STEPS = STAGES * HALF_GROUPS

SETUP = {}
_at = 0
for _n, _w in (("wdq", 128), ("wuq", 128), ("wdkv", 256), ("wuk", 256), ("wkr", 128), ("wqr", 128),
               ("wuv", 256), ("wo", 128), ("wk", 256), ("bias", 256)):
    SETUP[_n] = (_at, _at + _w)
    _at += _w
SETUP_W = _at
KEEP = {}
_at = 0
for _n, _w in (("pos", 256), ("wq", 256), ("wu", 256), ("b1", 32), ("bu", 1), ("ident", 128),
               ("block", HC), ("causal", T)):
    KEEP[_n] = (_at, _at + _w)
    _at += _w
KEEP_W = _at


def build(nc, x, wtok, setup, keep, w1, w2, b2, out, h2s, ws):
    with ExitStack() as ctx:
        def sb(name, shape, dt=F32):
            return ctx.enter_context(nc.sbuf_tensor(name, shape, dt))

        def sem(name):
            return ctx.enter_context(nc.semaphore(name))

        keep_sb = sb("keep_sb", [P, KEEP_W])
        raw = sb("raw", [P, 2048])
        xt = sb("xt", [P, XR, KF, P])
        wtok_sb = sb("wtok_sb", [P, KF, D])
        wbd = sb("wbd", [P, 4, P])
        u_sb = sb("u_sb", [P, 2, P])
        wqk = sb("wqk", [P, D])
        b2_sb = sb("b2_sb", [P, E, D])
        w1h = [sb(f"w1h{i}", [P, NC_, FF], F32R) for i in range(2)]
        w1l = [sb(f"w1l{i}", [P, NC_, FF], F32R) for i in range(2)]
        w2h = [sb(f"w2h{i}", [P, FC, D], F32R) for i in range(2)]
        w2l = [sb(f"w2l{i}", [P, FC, D], F32R) for i in range(2)]
        hid_h = sb("hid_h", [P, FC, HT], F32R)
        hid_l = sb("hid_l", [P, FC, HT], F32R)
        hid = sb("hid", [P, 2, HT])
        x2t_h = sb("x2t_h", [P, NC_, 2, HT], F32R)
        x2t_l = sb("x2t_l", [P, NC_, 2, HT], F32R)
        acc = sb("acc", [P, 2 * CLS, D])
        wcls = sb("wcls", [P, 2 * CLS, 4])
        hres = sb("hres", [P, 4, D])
        normed = sb("normed", [P, 4, D])
        kbuf = sb("kbuf", [P, 4, D])
        tbuf = sb("tbuf", [P, 4, 2, P])
        qkt = sb("qkt", [P, 4, 4, P])
        vx = sb("vx", [P, 4, H, HD + 1])
        bd = sb("bd", [P, 2, 2, HC, P])
        sq = bd[:, :, 0, :, :].rearrange("p r h t -> p r (h t)")[:, :, 0:2 * D].rearrange("p r (c f) -> p r c f", c=2)
        bnst = sb("bnst", [P, 4, 6])
        mv = sb("mv", [P, 2 * GROUPS, 2])
        ve = sb("ve", [P, 2 * GROUPS])
        rstd = sb("rstd", [P, 2 * GROUPS])
        neghalf = sb("neghalf", [P, 2 * H])
        ssq = sb("ssq", [P, 4, 2 * H])
        rinv = sb("rinv", [P, 4, 2 * H])
        mx = sb("mx", [P, 4, 2 * GI])
        rsum = sb("rsum", [P, 4, H])
        zr = sb("zr", [P, GROUPS])
        zt = sb("zt", [P, GROUPS])
        ez = sb("ez", [P, GROUPS])
        uu = sb("uu", [P, GROUPS])
        wmix = sb("wmix", [P, GROUPS, 4])

        def kp(name):
            a, b = KEEP[name]
            return keep_sb[:, a:b]

        def st(name, rows=P):
            a, b = SETUP[name]
            return raw[0:rows, a:b]

        bank = [ctx.enter_context(nc.psum_tensor(f"bank{i}", [P, 512], F32)) for i in range(8)]
        projb = bank

        ld_keep, ld_setup, ld_wtok, ld_b2 = sem("ld_keep"), sem("ld_setup"), sem("ld_wtok"), sem("ld_b2")
        ld_x = [sem(f"ld_x{i}") for i in range(XR)]
        ld_raw = sem("ld_raw")
        ld_acc = [sem(f"ld_acc{i}") for i in range(2)]
        st_h2 = [sem(f"st_h2{i}") for i in range(4)]
        st_w = sem("st_w")
        st_out = sem("st_out")
        setup_pe, setup_u, setup_done, ones_ready = sem("setup_pe"), sem("setup_u"), sem("setup_done"), sem("ones_ready")
        patch_done, hnt_done, proj_done, qkt_done = sem("patch_done"), sem("hnt_done"), sem("proj_done"), sem("qkt_done")
        score_done, pt_done, ctx_done, x2t_done = sem("score_done"), sem("pt_done"), sem("ctx_done"), sem("x2t_done")
        stats_ready, hn_ready, hnt_ready = sem("stats_ready"), sem("hn_ready"), sem("hnt_ready")
        sq_ready, v_ready, ssq_ready, rinv_ready = sem("sq_ready"), sem("v_ready"), sem("ssq_ready"), sem("rinv_ready")
        qk_ready, qkt_ready = sem("qk_ready"), sem("qkt_ready")
        qbd0_ready, qbd1_ready = sem("qbd0_ready"), sem("qbd1_ready")
        s_ready, p_ready, pt_ready = sem("s_ready"), sem("p_ready"), sem("pt_ready")
        pbd0_ready, pbd1_ready = sem("pbd0_ready"), sem("pbd1_ready")
        stats2_ready, x2_ready = sem("stats2_ready"), sem("x2_ready")
        x2th_ready, x2tl_ready = sem("x2th_ready"), sem("x2tl_ready")
        z_ready, ez_ready, wmix_ready = sem("z_ready"), sem("ez_ready"), sem("wmix_ready")
        wh_ready, wl_ready = sem("wh_ready"), sem("wl_ready")
        l1_done, hid_ready, hidh_ready, hidl_ready = sem("l1_done"), sem("hid_ready"), sem("hidh_ready"), sem("hidl_ready")
        l2_done, acc_ready = sem("l2_done"), sem("acc_ready")
        dve_chain, pool_chain = sem("dve_chain"), sem("pool_chain")

        def wslots(m):
            s = (m // 2) % 2
            hi, lo = ((w2h, w2l) if m % 2 else (w1h, w1l))
            return (hi[s][:, :, :].rearrange("p a b -> p (a b)"), lo[s][:, :, :].rearrange("p a b -> p (a b)"))

        EARLY = {8 + i: (i // 4, i % 4) for i in range(16)}

        def late_chunk(n, fc):
            if n in (3, 4):
                return (4 + 2 * (n - 3) + fc // 4, fc % 4)
            return None

        def wait_slot_free(eng, m):
            e = m // 2
            if e >= 2:
                n = UNITS.index((e - 2, 1))
                if m % 2 == 0:
                    eng.wait_ge(l1_done, FC * (n + 1))
                else:
                    eng.wait_ge(l2_done, 2 * (n + 1))

        def qbd(g, c):
            o = bd[:, g % 2, c, :, :].rearrange("p b (h q) -> p b h q", h=HC)
            a = qkt[:, g % 4, c, :].rearrange("p (b q) -> p b q", b=GI).unsqueeze(2).to_broadcast([P, GI, HC, T])
            m = kp("block").unsqueeze(1).unsqueeze(3).to_broadcast([P, GI, HC, T])
            return o, a, m

        def pbd(g, c):
            o = bd[:, g % 2, c, :, :].rearrange("p h (b q) -> p h b q", b=GI)
            a = tbuf[:, g % 4, c, :].rearrange("p (h q) -> p h q", h=HC).unsqueeze(2).to_broadcast([P, HC, GI, T])
            m = kp("block").unsqueeze(1).unsqueeze(3).to_broadcast([P, HC, GI, T])
            return o, a, m

        def wait_bd_free(eng, s, g):
            gg = g % 4
            if s == 3:
                if gg >= 2:
                    eng.wait_ge(score_done, g - 1)
                elif g >= 4:
                    eng.wait_ge(ctx_done, g - 1)
            elif gg < 2:
                eng.wait_ge(score_done, g + 3)
            else:
                eng.wait_ge(ctx_done, g - 1)

        block = ctx.enter_context(nc.Block())

        @block.sync
        def _(sp):
            def load_x(g):
                if g >= XR:
                    sp.wait_ge(patch_done, g - XR + 1)
                sp.dma_start(xt[:, g % XR, :, :], x[g]).then_inc(ld_x[g % XR], 16)

            def load_raw(m):
                if m == 0:
                    sp.wait_ge(setup_done, 1)
                else:
                    sp.wait_ge(wl_ready, 4 * m)
                e = m // 2
                if m % 2 == 0:
                    sp.dma_start(raw[:, :].rearrange("p (c f) -> p c f", c=NC_),
                                 w1[e].rearrange("(c p) f -> p c f", p=P)).then_inc(ld_raw, 16)
                else:
                    sp.dma_start(raw[:, :].rearrange("p (c f) -> p c f", c=FC),
                                 w2[e].rearrange("(c p) f -> p c f", p=P)).then_inc(ld_raw, 16)

            def load_acc(hf):
                for gg in range(4):
                    sp.wait_ge(st_h2[gg], 16 * (hf + 1))
                sp.wait_ge(st_w, 16 * (hf + 1))
                rows = h2s[hf * HT:(hf + 1) * HT, :].rearrange("(b j i) d -> j b i d", j=CLS, i=4)
                wrows = ws[hf * HT:(hf + 1) * HT, :].rearrange("(b j i) d -> j b i d", j=CLS, i=4)
                for j in range(CLS):
                    sp.dma_start(acc[:, hf * CLS + j, :], rows[j]).then_inc(ld_acc[hf], 16)
                    sp.dma_start(wcls[:, hf * CLS + j, :], wrows[j]).then_inc(ld_acc[hf], 16)

            sp.dma_start(keep_sb[:, :], keep).then_inc(ld_keep, 16)
            sp.dma_start(raw[:, 0:SETUP_W], setup).then_inc(ld_setup, 16)
            load_x(0)
            sp.dma_start(wtok_sb[:, :, :], wtok).then_inc(ld_wtok, 16)
            load_x(1)
            load_x(2)
            load_raw(0)
            load_x(3)
            load_raw(1)
            sp.dma_start(b2_sb[:, :, :].rearrange("p e d -> p (e d)"), b2).then_inc(ld_b2, 16)
            load_x(4)
            load_raw(2)
            load_x(5)
            load_x(6)
            load_raw(3)
            load_acc(0)
            load_x(7)
            load_acc(1)
            for m in range(4, 2 * E):
                load_raw(m)
            orow = out.rearrange("b (i j) d -> j b i d", j=CLS)
            for hf in range(2):
                n = UNITS.index((E - 1, hf))
                for j in range(CLS):
                    sp.wait_ge(acc_ready, 2 * n + j // 2 + 1)
                    sp.dma_start(orow[j, hf * 32:(hf + 1) * 32], acc[:, hf * CLS + j, :]).then_inc(st_out, 16)
            sp.wait_ge(st_out, 16 * 2 * CLS)

        @block.tensor
        def _(pe):
            ident = kp("ident")

            def mm(o, a, b, first, last, group=True):
                return pe.matmul(o, a, b, start=first, stop=last, skip_group_check=not group)

            def setup_products():
                pe.wait_ge(ld_keep, 16)
                pe.wait_ge(ld_setup, 16)
                for c in range(2):
                    r = mm(bank[5][:, c * P:(c + 1) * P], st("wuv", HD)[:, c * P:(c + 1) * P], st("wo", HD), True, True)
                r.then_inc(setup_pe, 1)
                mm(bank[4][:, 0:P], st("wdq"), st("wuq"), True, True)
                for c in range(2):
                    mm(bank[4][:, P:2 * P], st("wdkv")[:, c * P:(c + 1) * P], st("wuk")[:, c * P:(c + 1) * P], c == 0, c == 1)
                mm(bank[4][:, 2 * P:3 * P], st("wkr", 64), st("wqr", 64), True, True)
                pe.wait_ge(setup_u, 1)
                for c in range(2):
                    r = mm(bank[4][:, 3 * P:4 * P], st("wdkv")[:, c * P:(c + 1) * P], u_sb[:, c, :], c == 0, c == 1)
                r.then_inc(setup_pe, 1)

            def step(s, g):
                gg, base = g % 4, g - g % 4
                if s == 0:
                    pe.wait_ge(ld_x[g % XR], 16 * (g // XR + 1))
                    if g == 0:
                        pe.wait_ge(ld_wtok, 16)
                    if g >= 4:
                        pe.wait_ge(x2tl_ready, g - 3)
                    for c in range(KF):
                        r = mm(bank[gg][:, 0:D], xt[:, g % XR, c, :], wtok_sb[:, c, :], c == 0, c == KF - 1)
                    r.then_inc(patch_done, 1)
                elif s == 1:
                    pe.wait_ge(hn_ready, g + 1)
                    for c in range(NC_):
                        r = pe.transpose(bank[gg][:, c * P:(c + 1) * P], normed[:, gg, c * P:(c + 1) * P], ident)
                    r.then_inc(hnt_done, 1)
                elif s == 2:
                    if g == 0:
                        pe.wait_ge(setup_done, 1)
                    pe.wait_ge(hnt_ready, base + 2 * (gg % 2) + 2 if gg < 2 else g + 1)
                    if gg >= 2:
                        pe.wait_ge(qk_ready, g - 1)
                    for c in range(NC_):
                        r = mm(bank[2 * (g % 2) + c][:, :], tbuf[:, gg, c, :],
                               wbd[:, :, :].rearrange("p a b -> p (a b)"), True, True)
                    r.then_inc(proj_done, 1)
                elif s == 3:
                    pe.wait_ge(qk_ready, base + 3 + gg // 2)
                    for c in range(NC_):
                        pe.transpose(bank[gg][:, c * P:(c + 1) * P], normed[:, gg, c * P:(c + 1) * P], ident)
                    for c in range(NC_):
                        r = pe.transpose(bank[gg][:, (2 + c) * P:(3 + c) * P], kbuf[:, gg, c * P:(c + 1) * P], ident)
                    r.then_inc(qkt_done, 1)
                elif s == 4:
                    pe.wait_ge(qbd0_ready, g + 1)
                    pe.wait_ge(qbd1_ready, g + 1)
                    for c in range(NC_):
                        for b in range(GI):
                            o = (c * GI + b) * T
                            r = mm(bank[gg][:, o:o + T], bd[:, g % 2, c, b, :],
                                   qkt[:, gg, 2 + c, b * T:(b + 1) * T], True, True)
                    r.then_inc(score_done, 1)
                elif s == 5:
                    pe.wait_ge(p_ready, g + 1)
                    for c in range(NC_):
                        r = pe.transpose(bank[gg][:, c * P:(c + 1) * P], kbuf[:, gg, c * P:(c + 1) * P], ident)
                    r.then_inc(pt_done, 1)
                elif s == 6:
                    pe.wait_ge(pbd0_ready, g + 1)
                    pe.wait_ge(pbd1_ready, g + 1)
                    for h in range(H):
                        r = mm(bank[gg][:, h * (HD + 1):(h + 1) * (HD + 1)], bd[:, g % 2, h // HC, h % HC, :],
                               vx[:, gg, h, :], True, True)
                    r.then_inc(ctx_done, 1)
                else:
                    pe.wait_ge(x2_ready, g + 1)
                    for c in range(NC_):
                        r = pe.transpose(bank[gg][:, c * P:(c + 1) * P], normed[:, gg, c * P:(c + 1) * P], ident)
                    r.then_inc(x2t_done, 1)

            def layer1(n, fc):
                e, hf = UNITS[n]
                k = n * FC + fc
                if fc == 0:
                    pe.wait_ge(wl_ready, 4 * (2 * e + 1))
                    pe.wait_ge(x2tl_ready, 4 * (hf + 1))
                if k >= 2:
                    pe.wait_ge(hid_ready, k - 1)
                f = slice(fc * P, (fc + 1) * P)
                ps = bank[4 + k % 2]
                for c in range(NC_):
                    mm(ps[:, :], w1h[e % 2][:, c, f], x2t_h[:, c, hf, :], c == 0, False)
                    mm(ps[:, :], w1h[e % 2][:, c, f], x2t_l[:, c, hf, :], False, False)
                    r = mm(ps[:, :], w1l[e % 2][:, c, f], x2t_h[:, c, hf, :], False, c == NC_ - 1)
                r.then_inc(l1_done, 1)

            def layer2(n, fc):
                e, hf = UNITS[n]
                if fc == 0:
                    pe.wait_ge(wl_ready, 4 * (2 * e + 2))
                    if n:
                        pe.wait_ge(acc_ready, 2 * n)
                pe.wait_ge(hidl_ready, n * FC + fc + 1)
                for j in range(CLS):
                    t = slice(j * P, (j + 1) * P)
                    o = bank[6 + j // 2][:, (j % 2) * D:(j % 2 + 1) * D]
                    mm(o, hid_h[:, fc, t], w2h[e % 2][:, fc, :], fc == 0 and j % 2 == 0, False, False)
                    mm(o, hid_h[:, fc, t], w2l[e % 2][:, fc, :], False, False, False)
                    r = mm(o, hid_l[:, fc, t], w2h[e % 2][:, fc, :], False, fc == FC - 1, False)
                    if fc == FC - 1 and j % 2:
                        r.then_inc(l2_done, 1)

            setup_products()
            for q in range(STEPS):
                step(q // 4, q % 4)
            for q in range(STEPS):
                (layer1 if q % 16 < FC else layer2)(q // 16, q % FC)
                step(q // 4, 4 + q % 4)
            for n in range(2, len(UNITS)):
                for fc in range(FC):
                    layer1(n, fc)
                for fc in range(FC):
                    layer2(n, fc)

        @block.scalar
        def _(act):
            def step(s, g):
                gg = g % 4
                if s == 1:
                    act.wait_ge(hnt_done, g + 1)
                    act.activation(tbuf[:, gg, :, :], bank[gg][:, 0:D].rearrange("p (a b) -> p a b", a=2),
                                   ACT.Copy).then_inc(hnt_ready, 1)
                elif s == 2:
                    act.wait_ge(proj_done, g + 1)
                    if g >= 2:
                        act.wait_ge(ssq_ready, g - 1)
                    for c in range(NC_):
                        r = act.activation(sq[:, g % 2, c, :], bank[2 * (g % 2) + c][:, 0:2 * P], ACT.Square)
                    r.then_inc(sq_ready, 1)
                    if g == 0:
                        act.wait_ge(ones_ready, 1)
                    for c in range(NC_):
                        r = act.activation(vx[:, gg, c * HC:(c + 1) * HC, 0:HD],
                                           bank[2 * (g % 2) + c][:, 3 * P:4 * P].rearrange("p (h d) -> p h d", h=HC),
                                           ACT.Copy)
                    r.then_inc(v_ready, 1)
                elif s == 3:
                    act.wait_ge(qkt_done, g + 1)
                    act.activation(qkt[:, gg, :, :], bank[gg][:, :].rearrange("p (a b) -> p a b", a=4),
                                   ACT.Copy).then_inc(qkt_ready, 1)
                elif s == 4:
                    act.wait_ge(s_ready, g + 1)
                    act.activation(kbuf[:, gg, :], kbuf[:, gg, :], ACT.Exp).then_inc(p_ready, 1)
                elif s == 5:
                    act.wait_ge(pt_done, g + 1)
                    act.activation(tbuf[:, gg, :, :], bank[gg][:, 0:D].rearrange("p (a b) -> p a b", a=2),
                                   ACT.Copy).then_inc(pt_ready, 1)
                elif s == 6:
                    act.wait_ge(stats2_ready, g + 1)
                    act.dma_start(h2s[g * P:(g + 1) * P, :], hres[:, gg, :]).then_inc(st_h2[gg], 16)
                elif s == 7:
                    act.wait_ge(x2t_done, g + 1)
                    for c in range(NC_):
                        r = act.activation(
                            x2t_h[:, c, g // 4, :].rearrange("p (j g b i) -> p g b j i", j=CLS, g=4, i=4)[:, gg],
                            bank[gg][:, c * P:(c + 1) * P].rearrange("p (b j i) -> p b j i", j=CLS, i=4), ACT.Copy)
                    r.then_inc(x2th_ready, 1)

            def routing(hf):
                gs = slice(4 * hf, 4 * hf + 4)
                act.wait_ge(z_ready, hf + 1)
                act.activation(ez[:, gs], zt[:, gs], ACT.Exp, scale=-1.0).then_inc(ez_ready, 1)
                act.wait_ge(wmix_ready, hf + 1)
                act.dma_start(ws[hf * HT:(hf + 1) * HT, :].rearrange("(g p) i -> p g i", p=P),
                              wmix[:, gs, :]).then_inc(st_w, 16)

            def split_hi(m, quarter):
                act.wait_ge(ld_raw, 16 * (m + 1))
                wait_slot_free(act, m)
                f = slice(quarter * 512, (quarter + 1) * 512)
                act.activation(wslots(m)[0][:, f], raw[:, f], ACT.Copy).then_inc(wh_ready, 1)

            def hidden(n, fc):
                e, _ = UNITS[n]
                k = n * FC + fc
                act.wait_ge(l1_done, k + 1)
                if k >= 2:
                    act.wait_ge(hidl_ready, k - 1)
                act.activation(hid[:, k % 2, :], bank[4 + k % 2][:, :], ACT.Relu,
                               bias=kp("b1")[:, e * FC + fc:e * FC + fc + 1]).then_inc(hid_ready, 1)

            for q in range(STEPS):
                step(q // 4, q % 4)
                if q in EARLY:
                    split_hi(*EARLY[q])
            routing(0)
            for q in range(STEPS):
                if q % 16 < FC:
                    hidden(q // 16, q % FC)
                step(q // 4, 4 + q % 4)
            routing(1)
            for n in range(2, len(UNITS)):
                for fc in range(FC):
                    hidden(n, fc)
                    if late_chunk(n, fc):
                        split_hi(*late_chunk(n, fc))

        @block.gpsimd
        def _(pool):
            chained = [0]

            def link(ins):
                chained[0] += 1
                ins.then_inc(pool_chain, 1)
                pool.wait_ge(pool_chain, chained[0])

            def rsqrt(o, a, w):
                return pool.tensor_tensor(o, a, neghalf[:, 0:w], ALU.pow)

            def normalise(g, at, ready):
                gg = g % 4
                link(rsqrt(rstd[:, at:at + 1], ve[:, at:at + 1], 1))
                pool.tensor_scalar(normed[:, gg, :], hres[:, gg, :], mv[:, at, 0:1], rstd[:, at:at + 1],
                                   ALU.subtract, ALU.mult).then_inc(ready, 1)

            def spread(g, src, ready):
                pool.tensor_tensor(*src(g, 1), ALU.mult).then_inc(ready, 1)

            def step(s, g):
                gg = g % 4
                if s == 0:
                    pool.wait_ge(stats_ready, g + 1)
                    normalise(g, g, hn_ready)
                elif s == 2:
                    pool.wait_ge(ssq_ready, g + 1)
                    rsqrt(rinv[:, gg, :], ssq[:, gg, :], 2 * H).then_inc(rinv_ready, 1)
                elif s == 3:
                    pool.wait_ge(qkt_ready, g + 1)
                    wait_bd_free(pool, s, g)
                    spread(g, qbd, qbd1_ready)
                elif s == 5:
                    pool.wait_ge(pt_ready, g + 1)
                    wait_bd_free(pool, s, g)
                    spread(g, pbd, pbd1_ready)
                elif s == 6:
                    pool.wait_ge(stats2_ready, g + 1)
                    normalise(g, GROUPS + g, x2_ready)

            def split_lo(m, quarter):
                pool.wait_ge(wh_ready, 4 * m + quarter + 1)
                hi, lo = wslots(m)
                f = slice(quarter * 512, (quarter + 1) * 512)
                pool.tensor_tensor(lo[:, f], raw[:, f], hi[:, f].bitcast(F32), ALU.subtract).then_inc(wl_ready, 1)

            def hidden_hi(n, fc):
                k = n * FC + fc
                pool.wait_ge(hid_ready, k + 1)
                pool.tensor_copy(hid_h[:, fc, :], hid[:, k % 2, :]).then_inc(hidh_ready, 1)

            pool.memset(neghalf[:, :], -0.5).then_inc(ones_ready, 1)
            link(pool.memset(vx[:, :, :, :].rearrange("p a b c -> p (a b c)"), 1.0))
            for q in range(STEPS):
                step(q // 4, q % 4)
                if q in EARLY:
                    split_lo(*EARLY[q])
            for q in range(STEPS):
                if q % 16 < FC:
                    hidden_hi(q // 16, q % FC)
                step(q // 4, 4 + q % 4)
            for n in range(2, len(UNITS)):
                for fc in range(FC):
                    hidden_hi(n, fc)
                    if late_chunk(n, fc):
                        split_lo(*late_chunk(n, fc))

        @block.vector
        def _(dve):
            chained = [0]

            def link(ins):
                chained[0] += 1
                ins.then_inc(dve_chain, 1)
                dve.wait_ge(dve_chain, chained[0])

            def setup_weights():
                dve.wait_ge(setup_pe, 1)
                dve.tensor_copy(u_sb[:, :, :].rearrange("p a b -> p (a b)"), bank[5][:, 0:2 * P]).then_inc(setup_u, 1)
                dve.wait_ge(ld_keep, 16)
                link(dve.tensor_tensor(kp("pos"), kp("pos"), st("bias"), ALU.add))
                link(dve.tensor_tensor(wqk[:, :], kp("wq"), st("wk"), ALU.mult))
                dve.wait_ge(setup_pe, 2)
                link(dve.tensor_tensor(wbd[:, :, :].rearrange("p n (h d) -> p n h d", h=HC),
                                       bank[4][:, :].rearrange("p (n h d) -> p n h d", n=4, h=HC),
                                       kp("block").unsqueeze(1).unsqueeze(3).to_broadcast([P, 4, HC, HD]), ALU.mult))
                dve.tensor_tensor(wbd[:, 2, :], wbd[:, 2, :], kp("wq")[:, 0:P], ALU.mult).then_inc(setup_done, 1)

            def stats(gg, at):
                link(dve.bn_stats(bnst[:, gg, :], hres[:, gg, :]))
                link(dve.bn_aggr(mv[:, at, :], bnst[:, gg, :]))
                return dve.tensor_scalar(ve[:, at:at + 1], mv[:, at, 1:2], LN_EPS, None, ALU.add)

            def heads(ap):
                return ap.rearrange("p (h d) -> p h d", d=HD)

            def norm_qk(g):
                gg = g % 4
                dve.wait_ge(rinv_ready, g + 1)
                dve.wait_ge(v_ready, g + 1)
                for c in range(NC_):
                    ps = bank[2 * (g % 2) + c]
                    f = slice(c * P, (c + 1) * P)
                    r0 = 2 * HC * c
                    rb = rinv[:, gg, r0:r0 + 2 * HC].unsqueeze(2).to_broadcast([P, 2 * HC, HD])
                    dve.tensor_tensor(heads(normed[:, gg, f]), heads(ps[:, 0:P]), rb[:, 0:HC], ALU.mult)
                    r = dve.tensor_tensor(heads(kbuf[:, gg, f]), heads(ps[:, P:2 * P]), rb[:, HC:2 * HC], ALU.mult)
                link(r)
                link(dve.tensor_tensor(kbuf[:, gg, :], kbuf[:, gg, :], wqk[:, :], ALU.mult))
                for c in range(NC_):
                    f = slice(c * P, (c + 1) * P)
                    r = dve.tensor_tensor(kbuf[:, gg, f], kbuf[:, gg, f], bank[2 * (g % 2) + c][:, 2 * P:3 * P], ALU.add)
                r.then_inc(qk_ready, 1)

            def step(s, g):
                gg = g % 4
                if s == 0:
                    dve.wait_ge(patch_done, g + 1)
                    if g >= 4:
                        dve.wait_ge(st_h2[gg], 16)
                    link(dve.tensor_tensor(hres[:, gg, :], bank[gg][:, 0:D], kp("pos"), ALU.add))
                    stats(gg, g).then_inc(stats_ready, 1)
                elif s == 2:
                    dve.wait_ge(sq_ready, g + 1)
                    link(dve.tensor_reduce(ssq[:, gg, :], sq[:, g % 2, :, :].rearrange("p c (h d) -> p (c h) d", d=HD),
                                           AXX, ALU.add))
                    dve.tensor_scalar(ssq[:, gg, :], ssq[:, gg, :], 1.0 / HD, RMS_EPS, ALU.mult,
                                      ALU.add).then_inc(ssq_ready, 1)
                    if gg:
                        norm_qk(g - 1)
                    if gg == 3:
                        norm_qk(g)
                elif s == 3:
                    dve.wait_ge(qkt_ready, g + 1)
                    wait_bd_free(dve, s, g)
                    dve.tensor_tensor(*qbd(g, 0), ALU.mult).then_inc(qbd0_ready, 1)
                elif s == 4:
                    dve.wait_ge(score_done, g + 1)
                    sc = kbuf[:, gg, :].rearrange("p (a k) -> p a k", k=T)
                    link(dve.scalar_tensor_tensor(sc, bank[gg][:, 0:D].rearrange("p (a k) -> p a k", k=T), SCALE,
                                                  kp("causal").unsqueeze(1).to_broadcast([P, 2 * GI, T]),
                                                  ALU.mult, ALU.add))
                    link(dve.tensor_reduce(mx[:, gg, :], sc, AXX, ALU.max))
                    dve.tensor_tensor(sc, sc, mx[:, gg, :].unsqueeze(2).to_broadcast([P, 2 * GI, T]),
                                      ALU.subtract).then_inc(s_ready, 1)
                elif s == 5:
                    dve.wait_ge(pt_ready, g + 1)
                    wait_bd_free(dve, s, g)
                    dve.tensor_tensor(*pbd(g, 0), ALU.mult).then_inc(pbd0_ready, 1)
                elif s == 6:
                    dve.wait_ge(ctx_done, g + 1)
                    cx = bank[gg][:, 0:H * (HD + 1)].rearrange("p (h d) -> p h d", d=HD + 1)
                    link(dve.reciprocal(rsum[:, gg, :], cx[:, :, HD]))
                    link(dve.tensor_tensor(heads(kbuf[:, gg, :]), cx[:, :, 0:HD],
                                           rsum[:, gg, :].unsqueeze(2).to_broadcast([P, H, HD]), ALU.mult))
                    link(dve.tensor_tensor(hres[:, gg, :], hres[:, gg, :], kbuf[:, gg, :], ALU.add))
                    at = GROUPS + g
                    stats(gg, at).then_inc(stats2_ready, 1)
                    link(dve.scalar_tensor_tensor(kbuf[:, gg, :], hres[:, gg, :], mv[:, at, 0:1], kp("wu"),
                                                  ALU.subtract, ALU.mult, accum_out=zr[:, g:g + 1]))
                elif s == 7:
                    dve.wait_ge(x2th_ready, g + 1)
                    for c in range(NC_):
                        def cols(t):
                            return t[:, c, g // 4, :].rearrange("p (j g b i) -> p g b j i", j=CLS, g=4, i=4)[:, gg]
                        r = dve.tensor_tensor(cols(x2t_l), bank[gg][:, c * P:(c + 1) * P].rearrange(
                            "p (b j i) -> p b j i", j=CLS, i=4), cols(x2t_h).bitcast(F32), ALU.subtract)
                    r.then_inc(x2tl_ready, 1)

            def routing(hf):
                gs = slice(4 * hf, 4 * hf + 4)
                dve.wait_ge(x2_ready, 4 * (hf + 1))
                link(dve.tensor_tensor(zt[:, gs], zr[:, gs], rstd[:, GROUPS + 4 * hf:GROUPS + 4 * hf + 4], ALU.mult))
                dve.tensor_scalar(zt[:, gs], zt[:, gs], kp("bu"), None, ALU.add).then_inc(z_ready, 1)
                dve.wait_ge(ez_ready, hf + 1)
                link(dve.tensor_scalar(uu[:, gs], ez[:, gs], 1.0, None, ALU.add))
                link(dve.reciprocal(uu[:, gs], uu[:, gs]))
                for i in range(1, 4):
                    r = dve.tensor_scalar(wmix[:, gs, i], zt[:, gs], THRESH[i], 1.0 / (i + 1), ALU.is_gt, ALU.mult)
                link(r)
                for i in range(1, 4):
                    dve.tensor_tensor(wmix[:, gs, i], wmix[:, gs, i], uu[:, gs], ALU.mult)
                dve.tensor_copy(wmix[:, gs, 0], uu[:, gs]).then_inc(wmix_ready, 1)

            def hidden_lo(n, fc):
                k = n * FC + fc
                dve.wait_ge(hidh_ready, k + 1)
                dve.tensor_tensor(hid_l[:, fc, :], hid[:, k % 2, :], hid_h[:, fc, :].bitcast(F32),
                                  ALU.subtract).then_inc(hidl_ready, 1)

            def mix(n):
                e, hf = UNITS[n]

                def w(j):
                    i = (e - j) % 4
                    return wcls[:, hf * CLS + j, i:i + 1]
                if e == 0:
                    dve.wait_ge(ld_acc[hf], 16 * 2 * CLS)
                    if hf == 0:
                        dve.wait_ge(ld_b2, 16)
                for j in range(CLS):
                    a = acc[:, hf * CLS + j, :]
                    r = dve.scalar_tensor_tensor(a, b2_sb[:, e, :], w(j), a, ALU.mult, ALU.add)
                link(r)
                for j in range(CLS):
                    if j % 2 == 0:
                        dve.wait_ge(l2_done, 2 * n + j // 2 + 1)
                    a = acc[:, hf * CLS + j, :]
                    r = dve.scalar_tensor_tensor(a, bank[6 + j // 2][:, (j % 2) * D:(j % 2 + 1) * D], w(j), a,
                                                 ALU.mult, ALU.add)
                    if j % 2:
                        r.then_inc(acc_ready, 1)

            setup_weights()
            for q in range(STEPS):
                step(q // 4, q % 4)
            routing(0)
            for q in range(STEPS):
                if q % 16 < FC:
                    hidden_lo(q // 16, q % FC)
                step(q // 4, 4 + q % 4)
                if q == 17:
                    mix(0)
            routing(1)
            mix(1)
            for n in range(2, len(UNITS)):
                for fc in range(FC):
                    hidden_lo(n, fc)
                dve.wait_ge(acc_ready, 2 * n)
                mix(n)


def kernel(**inputs):
    import concourse.bacc as bacc
    from concourse.bass_utils import run_bass_kernel_spmd

    a = {k: np.ascontiguousarray(v) for k, v in inputs.items()}

    x = a["x"].reshape(GROUPS, GI, 3, 4, 16, 4, 16)
    x = x.transpose(0, 2, 4, 6, 1, 5, 3).reshape(GROUPS, KF, P, P)
    x = np.ascontiguousarray(x.transpose(0, 2, 1, 3))
    wtok = np.ascontiguousarray(a["L0_tok_W"].reshape(D, KF, P).transpose(2, 1, 0))
    at = {k[len("L0_attn_"):]: v for k, v in a.items() if k.startswith("L0_attn_")}

    def chunks(w):
        return w.reshape(2, P, -1).transpose(1, 0, 2).reshape(P, -1)

    def rows(v):
        return np.broadcast_to(v.reshape(1, -1), (P, v.size))

    f32 = np.float32
    setup = np.zeros((P, SETUP_W), f32)
    keep = np.zeros((P, KEEP_W), f32)

    def put(t, where, name, v):
        s = where[name][0]
        t[:v.shape[0], s:s + v.shape[1]] = v
    put(setup, SETUP, "wdq", np.tile(at["W_DQ"], (1, HC)))
    put(setup, SETUP, "wuq", np.tile(at["W_UQ"].T, (1, HC)))
    put(setup, SETUP, "wdkv", chunks(np.tile(at["W_DKV"], (1, HC))))
    put(setup, SETUP, "wuk", chunks(np.tile(at["W_UKV"][:HD].T, (1, HC))))
    put(setup, SETUP, "wkr", np.tile(at["W_KR"], (1, HC)))
    put(setup, SETUP, "wqr", np.tile(at["W_QR"], (1, HC)))
    put(setup, SETUP, "wuv", at["W_UKV"][HD:])
    put(setup, SETUP, "wo", np.tile(at["W_O"].T, (1, HC)))
    put(setup, SETUP, "wk", rows(np.tile(at["k_norm_w"], H)))
    put(setup, SETUP, "bias", rows(a["L0_tok_b"]))
    pos = a["L0_tok_pos_emb"].reshape(4, 4, D).transpose(1, 0, 2).reshape(T, D)
    put(keep, KEEP, "pos", np.tile(pos, (GI, 1)))
    put(keep, KEEP, "wq", rows(np.tile(at["q_norm_w"], H)))
    put(keep, KEEP, "wu", rows(a["L0_ffn_Wu"]))
    put(keep, KEEP, "b1", a["L0_ffn_b1"].reshape(E * FC, P).T)
    put(keep, KEEP, "bu", rows(a["L0_ffn_bu"]))
    part = np.arange(P)
    put(keep, KEEP, "ident", np.eye(P, dtype=f32))
    put(keep, KEEP, "block", (part[:, None] // T == np.arange(HC)[None]).astype(f32))
    order = np.arange(T)
    s_of = 4 * (order % 4) + order // 4
    put(keep, KEEP, "causal", np.where(s_of[None] <= s_of[part % T][:, None], 0.0, MASKED).astype(f32))
    b2 = rows(a["L0_ffn_b2"].reshape(-1))

    nc = bacc.Bacc("TRN2", target_bir_lowering=False, num_devices=1)
    arrays = {"x_t": x, "wtok_t": wtok, "setup": setup, "keep": keep, "w1": a["L0_ffn_W1"], "w2": a["L0_ffn_W2"],
              "b2_rows": np.ascontiguousarray(b2)}
    aps = [nc.dram_tensor(n, v.shape, mybir.dt.from_np(v.dtype), kind="ExternalInput").ap() for n, v in arrays.items()]
    out = nc.dram_tensor("out", (IMGS, T, D), F32, kind="ExternalOutput").ap()
    h2s = nc.dram_tensor("h2_rows", (TOK, D), F32, kind="Internal").ap()
    ws = nc.dram_tensor("mix_rows", (TOK, 4), F32, kind="Internal").ap()
    build(nc, *aps, out, h2s, ws)
    r = run_bass_kernel_spmd(nc, [arrays], core_ids=[0])
    return r.results[0]["out"]
```

```python
from contextlib import ExitStack

import numpy as np
import concourse.bass as bass
from concourse import mybir

F32 = mybir.dt.float32
F32R = mybir.dt.float32r
BF16 = mybir.dt.bfloat16
FP16 = mybir.dt.float16
ALU = mybir.AluOpType
ACT = mybir.ActivationFunctionType
AXX = mybir.AxisListType.X

P = 128
D = 256
NC_ = D // P
H, HD = 16, 16
HC = P // HD
T = 16
IMGS = 64
TOK = IMGS * T
GROUPS = TOK // P
GI = P // T
HALF_GROUPS = GROUPS // 2
HT = TOK // 2
KF = 768 // P
E = 4
FF = 1024
FC = FF // P
CLS = 4
LN_EPS = 1e-5
RMS_EPS = 1.1920929e-07
SCALE = HD ** -0.5
MASKED = -1e30
LN3 = float(np.log(3.0))
PARTS = [(0, 0), (0, 1), (0, 2), (1, 0), (1, 1)]
THRESH = [None, -LN3, 0.0, LN3]
XR = 2
UNITS = [(0, 0), (1, 0), (0, 1), (1, 1), (2, 0), (2, 1), (3, 0), (3, 1)]
STAGES = 8
STEPS = STAGES * HALF_GROUPS

SETUP = {}
_at = 0
for _n, _w in (("wdq", 128), ("wuq", 128), ("wdkv", 256), ("wuk", 256), ("wkr", 128), ("wqr", 128),
               ("wuv", 256), ("wo", 128), ("wk", 256), ("bias", 256)):
    SETUP[_n] = (_at, _at + _w)
    _at += _w
SETUP_W = _at
KEEP = {}
_at = 0
for _n, _w in (("pos", 256), ("wq", 256), ("wu", 256), ("b1", 32), ("bu", 1), ("ident", 128),
               ("block", HC), ("causal", T), ("eps", 2)):
    KEEP[_n] = (_at, _at + _w)
    _at += _w
KEEP_W = _at


def build(nc, x, wtok, setup, keep, w1, w2, b2, out, h2s, ws):
    with ExitStack() as ctx:
        def sb(name, shape, dt=F32):
            return ctx.enter_context(nc.sbuf_tensor(name, shape, dt))

        def sem(name):
            return ctx.enter_context(nc.semaphore(name))

        keep_sb = sb("keep_sb", [P, KEEP_W])
        raw = sb("raw", [P, 2048])
        xt = sb("xt", [P, XR, KF, P])
        wtok_sb = sb("wtok_sb", [P, KF, D])
        wbd = sb("wbd", [P, 4, P])
        b2_sb = sb("b2_sb", [P, E, D])
        w1h = [sb(f"w1h{i}", [P, NC_, FF], F32R) for i in range(2)]
        w1l = [sb(f"w1l{i}", [P, NC_, FF], F32R) for i in range(2)]
        w2h = [sb(f"w2h{i}", [P, FC, D], F32R) for i in range(2)]
        w2l = [sb(f"w2l{i}", [P, FC, D], F32R) for i in range(2)]
        hid_h = sb("hid_h", [P, FC, HT], F32R)
        hid_l = sb("hid_l", [P, FC, HT], F32R)
        hid = sb("hid", [P, 2, HT])
        x2t_h = sb("x2t_h", [P, NC_, 2, HT], F32R)
        x2t_l = sb("x2t_l", [P, NC_, 2, HT], F32R)
        acc = sb("acc", [P, 2 * CLS, D])
        wcls = sb("wcls", [P, 2 * CLS, 4])
        hres = sb("hres", [P, 4, D])
        normed = sb("normed", [P, 4, D])
        kbuf = sb("kbuf", [P, 4, D])
        tbuf = sb("tbuf", [P, 4, 2, P])
        u_sb = tbuf[:, 3, :, :]
        wqk = keep_sb[:, KEEP["wq"][0]:KEEP["wq"][1]]
        sp16 = sb("sp16", [P, 4, 2, 2, P], FP16)
        kt3 = sb("kt3", [P, 4, 3, 2, P], BF16)
        v3 = sb("v3", [P, 4, 3, H, HD + 1], BF16)
        bd = sb("bd", [P, 2, 4, HC, P], FP16)
        sq = bd[:, :, :, :, :].rearrange("p r a h t -> p r (a h t)").bitcast(F32)[:, :, 0:2 * D].rearrange(
            "p r (c f) -> p r c f", c=2)
        bnst = sb("bnst", [P, 4, 6])
        mv = sb("mv", [P, 2 * GROUPS, 2])
        rstd = sb("rstd", [P, 2 * GROUPS])
        ssq = sb("ssq", [P, 4, 2 * H])
        rinv = sb("rinv", [P, 4, 2 * H])
        mx = sb("mx", [P, 4, 2 * GI])
        rsum = sb("rsum", [P, 4, H])
        zr = sb("zr", [P, GROUPS])
        zt = sb("zt", [P, GROUPS])
        ez = sb("ez", [P, GROUPS])
        uu = sb("uu", [P, GROUPS])
        wmix = sb("wmix", [P, GROUPS, 4])

        def kp(name):
            a, b = KEEP[name]
            return keep_sb[:, a:b]

        def st(name, rows=P):
            a, b = SETUP[name]
            return raw[0:rows, a:b]

        psum = ctx.enter_context(nc.psum_tensor("psum", [P, 8, 512], F32))
        bank = [psum[:, i, :] for i in range(8)]

        def proj_banks(g):
            return psum[:, 2 * (g % 2):2 * (g % 2) + 2, :]

        ld_keep, ld_setup, ld_wtok, ld_b2 = sem("ld_keep"), sem("ld_setup"), sem("ld_wtok"), sem("ld_b2")
        ld_x = [sem(f"ld_x{i}") for i in range(XR)]
        ld_raw = sem("ld_raw")
        ld_acc = [sem(f"ld_acc{i}") for i in range(2)]
        st_h2 = [sem(f"st_h2{i}") for i in range(4)]
        st_w = sem("st_w")
        st_out = sem("st_out")
        setup_pe, setup_u, setup_done, ones_ready = sem("setup_pe"), sem("setup_u"), sem("setup_done"), sem("ones_ready")
        patch_done, hnt_done, proj_done, qkt_done = sem("patch_done"), sem("hnt_done"), sem("proj_done"), sem("qkt_done")
        score_done, pt_done, ctx_done, x2t_done = sem("score_done"), sem("pt_done"), sem("ctx_done"), sem("x2t_done")
        stats_ready, std_ready, hn_ready, hnt_ready = sem("stats_ready"), sem("std_ready"), sem("hn_ready"), sem("hnt_ready")
        sq_ready, va_ready, vrest_ready, v_ready = sem("sq_ready"), sem("va_ready"), sem("vrest_ready"), sem("v_ready")
        ssq_ready, rms_ready, qk_ready = sem("ssq_ready"), sem("rms_ready"), sem("qk_ready")
        qka_ready, krest_ready, k_ready = sem("qka_ready"), sem("krest_ready"), sem("k_ready")
        qbd_ready, pbd_ready = sem("qbd_ready"), sem("pbd_ready")
        s_ready, p_ready, pta_ready = sem("s_ready"), sem("p_ready"), sem("pta_ready")
        stats2_ready, std2_ready, x2_ready = sem("stats2_ready"), sem("std2_ready"), sem("x2_ready")
        x2th_ready, x2tl_ready = sem("x2th_ready"), sem("x2tl_ready")
        z_ready, ez_ready, wmix_ready = sem("z_ready"), sem("ez_ready"), sem("wmix_ready")
        wh_ready, wl_ready = sem("wh_ready"), sem("wl_ready")
        l1_done, hid_ready, hidl_ready = sem("l1_done"), sem("hid_ready"), sem("hidl_ready")
        l2_done, acc_ready = sem("l2_done"), sem("acc_ready")
        dve_chain, pool_chain = sem("dve_chain"), sem("pool_chain")

        def wslots(m):
            s = (m // 2) % 2
            hi, lo = ((w2h, w2l) if m % 2 else (w1h, w1l))
            return (hi[s][:, :, :].rearrange("p a b -> p (a b)"), lo[s][:, :, :].rearrange("p a b -> p (a b)"))

        EARLY = {8 + i: (i // 4, i % 4) for i in range(16)}

        def late_chunk(n, fc):
            if n in (3, 4):
                return (4 + 2 * (n - 3) + fc // 4, fc % 4)
            return None

        def wait_slot_free(eng, m):
            e = m // 2
            if e >= 2:
                n = UNITS.index((e - 2, 1))
                if m % 2 == 0:
                    eng.wait_ge(l1_done, FC * (n + 1))
                else:
                    eng.wait_ge(l2_done, 2 * (n + 1))

        def wait_bd_free(eng, s, g):
            gg = g % 4
            if s == 3:
                if gg >= 2:
                    eng.wait_ge(score_done, g - 1)
                elif g >= 4:
                    eng.wait_ge(ctx_done, g - 1)
            elif gg < 2:
                eng.wait_ge(score_done, g + 3)
            else:
                eng.wait_ge(ctx_done, g - 1)

        block = ctx.enter_context(nc.Block())

        @block.sync
        def _(sp):
            def load_x(g):
                if g >= XR:
                    sp.wait_ge(patch_done, g - XR + 1)
                sp.dma_start(xt[:, g % XR, :, :], x[g]).then_inc(ld_x[g % XR], 16)

            def load_raw(m):
                if m == 0:
                    sp.wait_ge(setup_done, 1)
                else:
                    sp.wait_ge(wl_ready, 4 * m)
                e = m // 2
                if m % 2 == 0:
                    sp.dma_start(raw[:, :].rearrange("p (c f) -> p c f", c=NC_),
                                 w1[e].rearrange("(c p) f -> p c f", p=P)).then_inc(ld_raw, 16)
                else:
                    sp.dma_start(raw[:, :].rearrange("p (c f) -> p c f", c=FC),
                                 w2[e].rearrange("(c p) f -> p c f", p=P)).then_inc(ld_raw, 16)

            def load_acc(hf):
                for gg in range(4):
                    sp.wait_ge(st_h2[gg], 16 * (hf + 1))
                sp.wait_ge(st_w, 16 * (hf + 1))
                rows = h2s[hf * HT:(hf + 1) * HT, :].rearrange("(b j i) d -> j b i d", j=CLS, i=4)
                wrows = ws[hf * HT:(hf + 1) * HT, :].rearrange("(b j i) d -> j b i d", j=CLS, i=4)
                for j in range(CLS):
                    sp.dma_start(acc[:, hf * CLS + j, :], rows[j]).then_inc(ld_acc[hf], 16)
                    sp.dma_start(wcls[:, hf * CLS + j, :], wrows[j]).then_inc(ld_acc[hf], 16)

            sp.dma_start(keep_sb[:, :], keep).then_inc(ld_keep, 16)
            sp.dma_start(raw[:, 0:SETUP_W], setup).then_inc(ld_setup, 16)
            load_x(0)
            sp.dma_start(wtok_sb[:, :, :], wtok).then_inc(ld_wtok, 16)
            load_x(1)
            load_x(2)
            load_raw(0)
            load_x(3)
            load_raw(1)
            sp.dma_start(b2_sb[:, :, :].rearrange("p e d -> p (e d)"), b2).then_inc(ld_b2, 16)
            load_x(4)
            load_raw(2)
            load_x(5)
            load_raw(3)
            load_x(6)
            load_acc(0)
            load_x(7)
            load_acc(1)
            for m in range(4, 2 * E):
                load_raw(m)
            orow = out.rearrange("b (i j) d -> j b i d", j=CLS)
            for hf in range(2):
                n = UNITS.index((E - 1, hf))
                for j in range(CLS):
                    sp.wait_ge(acc_ready, 2 * n + j // 2 + 1)
                    sp.dma_start(orow[j, hf * 32:(hf + 1) * 32], acc[:, hf * CLS + j, :]).then_inc(st_out, 16)
            sp.wait_ge(st_out, 16 * 2 * CLS)

        @block.tensor
        def _(pe):
            ident = kp("ident")

            def mm(o, a, b, first, last, group=True):
                return pe.matmul(o, a, b, start=first, stop=last, skip_group_check=not group)

            def setup_products():
                pe.wait_ge(ld_keep, 16)
                pe.wait_ge(ld_setup, 16)
                for c in range(2):
                    r = mm(bank[5][:, c * P:(c + 1) * P], st("wuv", HD)[:, c * P:(c + 1) * P], st("wo", HD), True, True)
                r.then_inc(setup_pe, 1)
                mm(bank[4][:, 0:P], st("wdq"), st("wuq"), True, True)
                for c in range(2):
                    mm(bank[4][:, P:2 * P], st("wdkv")[:, c * P:(c + 1) * P], st("wuk")[:, c * P:(c + 1) * P], c == 0, c == 1)
                mm(bank[4][:, 2 * P:3 * P], st("wkr", 64), st("wqr", 64), True, True)
                pe.wait_ge(setup_u, 1)
                for c in range(2):
                    r = mm(bank[4][:, 3 * P:4 * P], st("wdkv")[:, c * P:(c + 1) * P], u_sb[:, c, :], c == 0, c == 1)
                r.then_inc(setup_pe, 1)

            def step(s, g):
                gg, base = g % 4, g - g % 4
                if s == 0:
                    pe.wait_ge(ld_x[g % XR], 16 * (g // XR + 1))
                    if g == 0:
                        pe.wait_ge(ld_wtok, 16)
                    if g >= 4:
                        pe.wait_ge(x2tl_ready, g - 3)
                    for c in range(KF):
                        r = mm(bank[gg][:, 0:D], xt[:, g % XR, c, :], wtok_sb[:, c, :], c == 0, c == KF - 1)
                    r.then_inc(patch_done, 1)
                elif s == 1:
                    pe.wait_ge(hn_ready, g + 1)
                    for c in range(NC_):
                        r = pe.transpose(bank[gg][:, c * P:(c + 1) * P], normed[:, gg, c * P:(c + 1) * P], ident)
                    r.then_inc(hnt_done, 1)
                elif s == 2:
                    if g == 0:
                        pe.wait_ge(setup_done, 1)
                    pe.wait_ge(hnt_ready, base + 2 * (gg % 2) + 2 if gg < 2 else g + 1)
                    if gg >= 2:
                        pe.wait_ge(qk_ready, g - 1)
                        pe.wait_ge(vrest_ready, g - 1)
                    for c in range(NC_):
                        r = mm(bank[2 * (g % 2) + c][:, :], tbuf[:, gg, c, :],
                               wbd[:, :, :].rearrange("p a b -> p (a b)"), True, True)
                    r.then_inc(proj_done, 1)
                elif s == 3:
                    pe.wait_ge(qk_ready, base + 3 + gg // 2)
                    pe.wait_ge(vrest_ready, base + 3 + gg // 2)
                    for c in range(NC_):
                        pe.transpose(bank[gg][:, c * P:(c + 1) * P], normed[:, gg, c * P:(c + 1) * P], ident)
                    for c in range(NC_):
                        r = pe.transpose(bank[gg][:, (2 + c) * P:(3 + c) * P], kbuf[:, gg, c * P:(c + 1) * P], ident)
                    r.then_inc(qkt_done, 1)
                elif s == 4:
                    pe.wait_ge(qbd_ready, g + 1)
                    pe.wait_ge(k_ready, g + 1)
                    for c in range(NC_):
                        for b in range(GI):
                            o = (c * GI + b) * T
                            for n, (a, m) in enumerate(PARTS):
                                r = mm(bank[gg][:, o:o + T], bd[:, g % 2, 2 * a + c, b, :],
                                       kt3[:, gg, m, c, b * T:(b + 1) * T], n == 0, n == len(PARTS) - 1)
                    r.then_inc(score_done, 1)
                elif s == 5:
                    pe.wait_ge(p_ready, g + 1)
                    for c in range(NC_):
                        r = pe.transpose(bank[gg][:, c * P:(c + 1) * P], kbuf[:, gg, c * P:(c + 1) * P], ident)
                    r.then_inc(pt_done, 1)
                elif s == 6:
                    pe.wait_ge(pbd_ready, g + 1)
                    pe.wait_ge(v_ready, g + 1)
                    for h in range(H):
                        c, hc = h // HC, h % HC
                        for n, (a, m) in enumerate(PARTS):
                            r = mm(bank[gg][:, h * (HD + 1):(h + 1) * (HD + 1)], bd[:, g % 2, 2 * a + c, hc, :],
                                   v3[:, gg, m, h, :], n == 0, n == len(PARTS) - 1)
                    r.then_inc(ctx_done, 1)
                else:
                    pe.wait_ge(x2_ready, g + 1)
                    for c in range(NC_):
                        r = pe.transpose(bank[gg][:, c * P:(c + 1) * P], normed[:, gg, c * P:(c + 1) * P], ident)
                    r.then_inc(x2t_done, 1)

            def layer1(n, fc):
                e, hf = UNITS[n]
                k = n * FC + fc
                if fc == 0:
                    pe.wait_ge(wl_ready, 4 * (2 * e + 1))
                    pe.wait_ge(x2tl_ready, 4 * (hf + 1))
                if k >= 2:
                    pe.wait_ge(hid_ready, k - 1)
                f = slice(fc * P, (fc + 1) * P)
                ps = bank[4 + k % 2]
                for c in range(NC_):
                    mm(ps[:, :], w1h[e % 2][:, c, f], x2t_h[:, c, hf, :], c == 0, False)
                    mm(ps[:, :], w1h[e % 2][:, c, f], x2t_l[:, c, hf, :], False, False)
                    r = mm(ps[:, :], w1l[e % 2][:, c, f], x2t_h[:, c, hf, :], False, c == NC_ - 1)
                r.then_inc(l1_done, 1)

            def layer2(n, fc):
                e, hf = UNITS[n]
                if fc == 0:
                    pe.wait_ge(wl_ready, 4 * (2 * e + 2))
                    if n:
                        pe.wait_ge(acc_ready, 2 * n)
                pe.wait_ge(hidl_ready, n * FC + fc + 1)
                for j in range(CLS):
                    t = slice(j * P, (j + 1) * P)
                    o = bank[6 + j // 2][:, (j % 2) * D:(j % 2 + 1) * D]
                    mm(o, hid_h[:, fc, t], w2h[e % 2][:, fc, :], fc == 0 and j % 2 == 0, False, False)
                    mm(o, hid_h[:, fc, t], w2l[e % 2][:, fc, :], False, False, False)
                    r = mm(o, hid_l[:, fc, t], w2h[e % 2][:, fc, :], False, fc == FC - 1, False)
                    if fc == FC - 1 and j % 2:
                        r.then_inc(l2_done, 1)

            setup_products()
            for q in range(STEPS):
                step(q // 4, q % 4)
            for q in range(STEPS):
                (layer1 if q % 16 < FC else layer2)(q // 16, q % FC)
                step(q // 4, 4 + q % 4)
            for n in range(2, len(UNITS)):
                for fc in range(FC):
                    layer1(n, fc)
                for fc in range(FC):
                    layer2(n, fc)

        @block.scalar
        def _(act):
            def two(ap):
                return ap.rearrange("p (a b) -> p a b", a=2)

            def std(at, ready, wait):
                act.wait_ge(*wait)
                act.activation(rstd[:, at:at + 1], mv[:, at, 1:2], ACT.Sqrt, bias=kp("eps")[:, 0:1]).then_inc(ready, 1)

            def step(s, g):
                gg = g % 4
                if s == 0:
                    if g == 0:
                        act.wait_ge(ld_keep, 16)
                    std(g, std_ready, (stats_ready, g + 1))
                elif s == 1:
                    act.wait_ge(hnt_done, g + 1)
                    act.activation(tbuf[:, gg, :, :], two(bank[gg][:, 0:D]), ACT.Copy).then_inc(hnt_ready, 1)
                elif s == 2:
                    act.wait_ge(proj_done, g + 1)
                    if g >= 2:
                        act.wait_ge(ssq_ready, g - 1)
                    ps = proj_banks(g)
                    act.activation(sq[:, g % 2, :, :], ps[:, :, 0:2 * P], ACT.Square).then_inc(sq_ready, 1)
                    if g == 0:
                        act.wait_ge(ones_ready, 1)
                    act.activation(v3[:, gg, 0, :, 0:HD].rearrange("p (c h) d -> p c h d", c=NC_),
                                   ps[:, :, 3 * P:4 * P].rearrange("p c (h d) -> p c h d", h=HC),
                                   ACT.Copy).then_inc(va_ready, 1)
                    act.wait_ge(ssq_ready, g + 1)
                    act.activation(rinv[:, gg, :], ssq[:, gg, :], ACT.Sqrt, scale=1.0 / HD,
                                   bias=kp("eps")[:, 1:2]).then_inc(rms_ready, 1)
                elif s == 3:
                    act.wait_ge(qkt_done, g + 1)
                    act.activation(sp16[:, gg, 0, :, :], two(bank[gg][:, 0:D]), ACT.Copy)
                    act.activation(kt3[:, gg, 0, :, :], two(bank[gg][:, D:2 * D]), ACT.Copy).then_inc(qka_ready, 1)
                elif s == 4:
                    act.wait_ge(s_ready, g + 1)
                    act.activation(kbuf[:, gg, :], kbuf[:, gg, :], ACT.Exp).then_inc(p_ready, 1)
                elif s == 5:
                    act.wait_ge(pt_done, g + 1)
                    act.activation(sp16[:, gg, 0, :, :], two(bank[gg][:, 0:D]), ACT.Copy).then_inc(pta_ready, 1)
                elif s == 6:
                    std(GROUPS + g, std2_ready, (stats2_ready, g + 1))
                    act.dma_start(h2s[g * P:(g + 1) * P, :], hres[:, gg, :]).then_inc(st_h2[gg], 16)
                elif s == 7:
                    act.wait_ge(x2t_done, g + 1)
                    for c in range(NC_):
                        r = act.activation(
                            x2t_h[:, c, g // 4, :].rearrange("p (j g b i) -> p g b j i", j=CLS, g=4, i=4)[:, gg],
                            bank[gg][:, c * P:(c + 1) * P].rearrange("p (b j i) -> p b j i", j=CLS, i=4), ACT.Copy)
                    r.then_inc(x2th_ready, 1)

            def routing(hf):
                gs = slice(4 * hf, 4 * hf + 4)
                act.wait_ge(z_ready, hf + 1)
                act.activation(ez[:, gs], zt[:, gs], ACT.Exp, scale=-1.0).then_inc(ez_ready, 1)
                act.wait_ge(wmix_ready, hf + 1)
                act.dma_start(ws[hf * HT:(hf + 1) * HT, :].rearrange("(g p) i -> p g i", p=P),
                              wmix[:, gs, :]).then_inc(st_w, 16)

            def split_hi(m, quarter):
                act.wait_ge(ld_raw, 16 * (m + 1))
                wait_slot_free(act, m)
                f = slice(quarter * 512, (quarter + 1) * 512)
                act.activation(wslots(m)[0][:, f], raw[:, f], ACT.Copy).then_inc(wh_ready, 1)

            def hidden(n, fc):
                e, _ = UNITS[n]
                k = n * FC + fc
                act.wait_ge(l1_done, k + 1)
                if k >= 2:
                    act.wait_ge(hidl_ready, k - 1)
                b1 = kp("b1")[:, e * FC + fc:e * FC + fc + 1]
                act.activation(hid_h[:, fc, :], bank[4 + k % 2][:, :], ACT.Relu, bias=b1)
                act.activation(hid[:, k % 2, :], bank[4 + k % 2][:, :], ACT.Relu, bias=b1).then_inc(hid_ready, 1)

            for q in range(STEPS):
                step(q // 4, q % 4)
                if q in EARLY:
                    split_hi(*EARLY[q])
            routing(0)
            for q in range(STEPS):
                if q % 16 < FC:
                    hidden(q // 16, q % FC)
                step(q // 4, 4 + q % 4)
            routing(1)
            for n in range(2, len(UNITS)):
                for fc in range(FC):
                    hidden(n, fc)
                    if late_chunk(n, fc):
                        split_hi(*late_chunk(n, fc))

        @block.gpsimd
        def _(pool):
            chained = [0]

            def link(ins):
                chained[0] += 1
                ins.then_inc(pool_chain, 1)
                pool.wait_ge(pool_chain, chained[0])

            def step(s, g):
                gg = g % 4
                if s == 2:
                    pool.wait_ge(vrest_ready, g + 1)
                    rest = tbuf[:, gg, :, :].rearrange("p c (h d) -> p (c h) d", d=HD)
                    link(pool.tensor_copy(v3[:, gg, 1, :, 0:HD], rest))
                    pool.tensor_tensor(v3[:, gg, 2, :, 0:HD], rest, v3[:, gg, 1, :, 0:HD], ALU.subtract).then_inc(v_ready, 1)
                elif s == 3:
                    pool.wait_ge(krest_ready, g + 1)
                    rest = kbuf[:, gg, :].rearrange("p (c t) -> p c t", c=NC_)
                    link(pool.tensor_copy(kt3[:, gg, 1, :, :], rest))
                    pool.tensor_tensor(kt3[:, gg, 2, :, :], rest, kt3[:, gg, 1, :, :], ALU.subtract).then_inc(k_ready, 1)

            def split_lo(m, quarter):
                pool.wait_ge(wh_ready, 4 * m + quarter + 1)
                hi, lo = wslots(m)
                f = slice(quarter * 512, (quarter + 1) * 512)
                pool.tensor_tensor(lo[:, f], raw[:, f], hi[:, f].bitcast(F32), ALU.subtract).then_inc(wl_ready, 1)

            link(pool.memset(v3[:, :, :, :, :].rearrange("p a b h d -> p (a b h d)"), 0.0))
            pool.memset(v3[:, :, 0, :, HD:HD + 1], 1.0).then_inc(ones_ready, 1)
            for q in range(STEPS):
                step(q // 4, q % 4)
                if q in EARLY:
                    split_lo(*EARLY[q])
            for q in range(STEPS):
                step(q // 4, 4 + q % 4)
            for n in range(2, len(UNITS)):
                for fc in range(FC):
                    if late_chunk(n, fc):
                        split_lo(*late_chunk(n, fc))

        @block.vector
        def _(dve):
            chained = [0]

            def link(ins):
                chained[0] += 1
                ins.then_inc(dve_chain, 1)
                dve.wait_ge(dve_chain, chained[0])

            def setup_weights():
                dve.wait_ge(setup_pe, 1)
                dve.tensor_copy(u_sb, bank[5][:, 0:2 * P].rearrange("p (a b) -> p a b", a=2)).then_inc(setup_u, 1)
                dve.wait_ge(ld_keep, 16)
                link(dve.tensor_tensor(kp("pos"), kp("pos"), st("bias"), ALU.add))
                dve.wait_ge(setup_pe, 2)
                link(dve.tensor_tensor(wbd[:, :, :].rearrange("p n (h d) -> p n h d", h=HC),
                                       bank[4][:, :].rearrange("p (n h d) -> p n h d", n=4, h=HC),
                                       kp("block").unsqueeze(1).unsqueeze(3).to_broadcast([P, 4, HC, HD]), ALU.mult))
                link(dve.tensor_tensor(wbd[:, 2, :], wbd[:, 2, :], kp("wq")[:, 0:P], ALU.mult))
                dve.tensor_tensor(wqk, kp("wq"), st("wk"), ALU.mult).then_inc(setup_done, 1)

            def stats(gg, at):
                link(dve.bn_stats(bnst[:, gg, :], hres[:, gg, :]))
                return dve.bn_aggr(mv[:, at, :], bnst[:, gg, :])

            def normalise(g, at, std, ready):
                gg = g % 4
                dve.wait_ge(std, g + 1)
                link(dve.reciprocal(rstd[:, at:at + 1], rstd[:, at:at + 1]))
                dve.tensor_scalar(normed[:, gg, :], hres[:, gg, :], mv[:, at, 0:1], rstd[:, at:at + 1],
                                  ALU.subtract, ALU.mult).then_inc(ready, 1)

            def late(g, last_step):
                if g % 4:
                    last_step(g - 1)
                if g % 4 == 3:
                    last_step(g)

            def spread_queries(g):
                a = sp16[:, g % 4, :, :, :].rearrange("p s c (b q) -> p (s c) b q", q=T)
                for h in range(HC):
                    r = dve.tensor_scalar(bd[:, g % 2, :, :, h * T:(h + 1) * T], a, kp("block")[:, h:h + 1], None, ALU.mult)
                r.then_inc(qbd_ready, 1)

            def spread_probabilities(g):
                a = sp16[:, g % 4, :, :, :].rearrange("p s c (h q) -> p (s c) h q", q=T)
                for b in range(GI):
                    r = dve.tensor_scalar(bd[:, g % 2, :, :, b * T:(b + 1) * T], a, kp("block")[:, b:b + 1], None, ALU.mult)
                r.then_inc(pbd_ready, 1)

            def heads(ap):
                return ap.rearrange("p (h d) -> p h d", d=HD)

            def chunked_heads(ap):
                return ap.rearrange("p c (h d) -> p c h d", d=HD)

            def norm_qk(g):
                gg = g % 4
                ps = proj_banks(g)
                dve.wait_ge(rms_ready, g + 1)
                link(dve.reciprocal(rinv[:, gg, :], rinv[:, gg, :]))
                rb = rinv[:, gg, :].rearrange("p (c a h) -> p c a h", c=NC_, a=2).unsqueeze(4).to_broadcast(
                    [P, NC_, 2, HC, HD])
                qn = normed[:, gg, :].rearrange("p (c h d) -> p c h d", c=NC_, d=HD)
                kn = kbuf[:, gg, :].rearrange("p (c h d) -> p c h d", c=NC_, d=HD)
                kn2 = kbuf[:, gg, :].rearrange("p (c f) -> p c f", c=NC_)
                link(dve.tensor_tensor(kn, chunked_heads(ps[:, :, P:2 * P]), rb[:, :, 1], ALU.mult))
                dve.tensor_tensor(qn, chunked_heads(ps[:, :, 0:P]), rb[:, :, 0], ALU.mult)
                link(dve.tensor_tensor(kbuf[:, gg, :], kbuf[:, gg, :], wqk, ALU.mult))
                dve.tensor_tensor(kn2, kn2, ps[:, :, 2 * P:3 * P], ALU.add).then_inc(qk_ready, 1)

            def step(s, g):
                gg = g % 4
                if s == 0:
                    dve.wait_ge(patch_done, g + 1)
                    if g >= 4:
                        dve.wait_ge(st_h2[gg], 16)
                    link(dve.tensor_tensor(hres[:, gg, :], bank[gg][:, 0:D], kp("pos"), ALU.add))
                    stats(gg, g).then_inc(stats_ready, 1)
                    late(g, lambda n: normalise(n, n, std_ready, hn_ready))
                elif s == 2:
                    dve.wait_ge(sq_ready, g + 1)
                    dve.tensor_reduce(ssq[:, gg, :], sq[:, g % 2, :, :].rearrange("p c (h d) -> p (c h) d", d=HD),
                                      AXX, ALU.add).then_inc(ssq_ready, 1)
                    dve.wait_ge(va_ready, g + 1)
                    dve.tensor_tensor(chunked_heads(tbuf[:, gg, :, :]), chunked_heads(proj_banks(g)[:, :, 3 * P:4 * P]),
                                      v3[:, gg, 0, :, 0:HD].rearrange("p (c h) d -> p c h d", c=NC_),
                                      ALU.subtract).then_inc(vrest_ready, 1)
                    late(g, norm_qk)
                elif s == 3:
                    dve.wait_ge(qka_ready, g + 1)
                    b2v = bank[gg][:, :].rearrange("p (n c t) -> p n c t", n=2, c=NC_)
                    dve.tensor_tensor(kbuf[:, gg, :].rearrange("p (c t) -> p c t", c=NC_), b2v[:, 1], kt3[:, gg, 0, :, :],
                                      ALU.subtract).then_inc(krest_ready, 1)
                    link(dve.tensor_tensor(sp16[:, gg, 1, :, :], b2v[:, 0], sp16[:, gg, 0, :, :], ALU.subtract))
                    wait_bd_free(dve, s, g)
                    spread_queries(g)
                elif s == 4:
                    dve.wait_ge(score_done, g + 1)
                    sc = kbuf[:, gg, :].rearrange("p (a k) -> p a k", k=T)
                    link(dve.scalar_tensor_tensor(sc, bank[gg][:, 0:D].rearrange("p (a k) -> p a k", k=T), SCALE,
                                                  kp("causal").unsqueeze(1).to_broadcast([P, 2 * GI, T]),
                                                  ALU.mult, ALU.add))
                    link(dve.tensor_reduce(mx[:, gg, :], sc, AXX, ALU.max))
                    dve.tensor_tensor(sc, sc, mx[:, gg, :].unsqueeze(2).to_broadcast([P, 2 * GI, T]),
                                      ALU.subtract).then_inc(s_ready, 1)
                elif s == 5:
                    dve.wait_ge(pta_ready, g + 1)
                    link(dve.tensor_tensor(sp16[:, gg, 1, :, :], bank[gg][:, 0:D].rearrange("p (c t) -> p c t", c=NC_),
                                           sp16[:, gg, 0, :, :], ALU.subtract))
                    wait_bd_free(dve, s, g)
                    spread_probabilities(g)
                elif s == 6:
                    dve.wait_ge(ctx_done, g + 1)
                    cx = bank[gg][:, 0:H * (HD + 1)].rearrange("p (h d) -> p h d", d=HD + 1)
                    link(dve.reciprocal(rsum[:, gg, :], cx[:, :, HD]))
                    link(dve.tensor_tensor(heads(kbuf[:, gg, :]), cx[:, :, 0:HD],
                                           rsum[:, gg, :].unsqueeze(2).to_broadcast([P, H, HD]), ALU.mult))
                    link(dve.tensor_tensor(hres[:, gg, :], hres[:, gg, :], kbuf[:, gg, :], ALU.add))
                    at = GROUPS + g
                    r = stats(gg, at)
                    r.then_inc(stats2_ready, 1)
                    dve.wait_ge(stats2_ready, g + 1)
                    dve.scalar_tensor_tensor(kbuf[:, gg, :], hres[:, gg, :], mv[:, at, 0:1], kp("wu"),
                                             ALU.subtract, ALU.mult, accum_out=zr[:, g:g + 1])
                    late(g, lambda n: normalise(n, GROUPS + n, std2_ready, x2_ready))
                elif s == 7:
                    dve.wait_ge(x2th_ready, g + 1)
                    for c in range(NC_):
                        def cols(t):
                            return t[:, c, g // 4, :].rearrange("p (j g b i) -> p g b j i", j=CLS, g=4, i=4)[:, gg]
                        r = dve.tensor_tensor(cols(x2t_l), bank[gg][:, c * P:(c + 1) * P].rearrange(
                            "p (b j i) -> p b j i", j=CLS, i=4), cols(x2t_h).bitcast(F32), ALU.subtract)
                    r.then_inc(x2tl_ready, 1)

            def routing(hf):
                gs = slice(4 * hf, 4 * hf + 4)
                dve.wait_ge(x2_ready, 4 * (hf + 1))
                link(dve.tensor_tensor(zt[:, gs], zr[:, gs], rstd[:, GROUPS + 4 * hf:GROUPS + 4 * hf + 4], ALU.mult))
                dve.tensor_scalar(zt[:, gs], zt[:, gs], kp("bu"), None, ALU.add).then_inc(z_ready, 1)
                dve.wait_ge(ez_ready, hf + 1)
                link(dve.tensor_scalar(uu[:, gs], ez[:, gs], 1.0, None, ALU.add))
                link(dve.reciprocal(uu[:, gs], uu[:, gs]))
                for i in range(1, 4):
                    r = dve.tensor_scalar(wmix[:, gs, i], zt[:, gs], THRESH[i], 1.0 / (i + 1), ALU.is_gt, ALU.mult)
                link(r)
                for i in range(1, 4):
                    dve.tensor_tensor(wmix[:, gs, i], wmix[:, gs, i], uu[:, gs], ALU.mult)
                dve.tensor_copy(wmix[:, gs, 0], uu[:, gs]).then_inc(wmix_ready, 1)

            def hidden_lo(n, fc):
                k = n * FC + fc
                dve.wait_ge(hid_ready, k + 1)
                dve.tensor_tensor(hid_l[:, fc, :], hid[:, k % 2, :], hid_h[:, fc, :].bitcast(F32),
                                  ALU.subtract).then_inc(hidl_ready, 1)

            def mix(n):
                e, hf = UNITS[n]

                def w(j):
                    i = (e - j) % 4
                    return wcls[:, hf * CLS + j, i:i + 1]
                if e == 0:
                    dve.wait_ge(ld_acc[hf], 16 * 2 * CLS)
                    if hf == 0:
                        dve.wait_ge(ld_b2, 16)
                for j in range(CLS):
                    a = acc[:, hf * CLS + j, :]
                    r = dve.scalar_tensor_tensor(a, b2_sb[:, e, :], w(j), a, ALU.mult, ALU.add)
                link(r)
                for j in range(CLS):
                    if j % 2 == 0:
                        dve.wait_ge(l2_done, 2 * n + j // 2 + 1)
                    a = acc[:, hf * CLS + j, :]
                    r = dve.scalar_tensor_tensor(a, bank[6 + j // 2][:, (j % 2) * D:(j % 2 + 1) * D], w(j), a,
                                                 ALU.mult, ALU.add)
                    if j % 2:
                        r.then_inc(acc_ready, 1)

            setup_weights()
            for q in range(STEPS):
                step(q // 4, q % 4)
            routing(0)
            for q in range(STEPS):
                if q % 16 < FC:
                    hidden_lo(q // 16, q % FC)
                step(q // 4, 4 + q % 4)
                if q == 17:
                    mix(0)
            routing(1)
            mix(1)
            for n in range(2, len(UNITS)):
                for fc in range(FC):
                    hidden_lo(n, fc)
                dve.wait_ge(acc_ready, 2 * n)
                mix(n)


def kernel(**inputs):
    import concourse.bacc as bacc
    from concourse.bass_utils import run_bass_kernel_spmd

    a = {k: np.ascontiguousarray(v) for k, v in inputs.items()}

    x = a["x"].reshape(GROUPS, GI, 3, 4, 16, 4, 16)
    x = x.transpose(0, 2, 4, 6, 1, 5, 3).reshape(GROUPS, KF, P, P)
    x = np.ascontiguousarray(x.transpose(0, 2, 1, 3))
    wtok = np.ascontiguousarray(a["L0_tok_W"].reshape(D, KF, P).transpose(2, 1, 0))
    at = {k[len("L0_attn_"):]: v for k, v in a.items() if k.startswith("L0_attn_")}

    def chunks(w):
        return w.reshape(2, P, -1).transpose(1, 0, 2).reshape(P, -1)

    def rows(v):
        return np.broadcast_to(v.reshape(1, -1), (P, v.size))

    f32 = np.float32
    setup = np.zeros((P, SETUP_W), f32)
    keep = np.zeros((P, KEEP_W), f32)

    def put(t, where, name, v):
        s = where[name][0]
        t[:v.shape[0], s:s + v.shape[1]] = v
    put(setup, SETUP, "wdq", np.tile(at["W_DQ"], (1, HC)))
    put(setup, SETUP, "wuq", np.tile(at["W_UQ"].T, (1, HC)))
    put(setup, SETUP, "wdkv", chunks(np.tile(at["W_DKV"], (1, HC))))
    put(setup, SETUP, "wuk", chunks(np.tile(at["W_UKV"][:HD].T, (1, HC))))
    put(setup, SETUP, "wkr", np.tile(at["W_KR"], (1, HC)))
    put(setup, SETUP, "wqr", np.tile(at["W_QR"], (1, HC)))
    put(setup, SETUP, "wuv", at["W_UKV"][HD:])
    put(setup, SETUP, "wo", np.tile(at["W_O"].T, (1, HC)))
    put(setup, SETUP, "wk", rows(np.tile(at["k_norm_w"], H)))
    put(setup, SETUP, "bias", rows(a["L0_tok_b"]))
    put(keep, KEEP, "eps", np.broadcast_to(np.array([LN_EPS, RMS_EPS], f32), (P, 2)))
    pos = a["L0_tok_pos_emb"].reshape(4, 4, D).transpose(1, 0, 2).reshape(T, D)
    put(keep, KEEP, "pos", np.tile(pos, (GI, 1)))
    put(keep, KEEP, "wq", rows(np.tile(at["q_norm_w"], H)))
    put(keep, KEEP, "wu", rows(a["L0_ffn_Wu"]))
    put(keep, KEEP, "b1", a["L0_ffn_b1"].reshape(E * FC, P).T)
    put(keep, KEEP, "bu", rows(a["L0_ffn_bu"]))
    part = np.arange(P)
    put(keep, KEEP, "ident", np.eye(P, dtype=f32))
    put(keep, KEEP, "block", (part[:, None] // T == np.arange(HC)[None]).astype(f32))
    order = np.arange(T)
    s_of = 4 * (order % 4) + order // 4
    put(keep, KEEP, "causal", np.where(s_of[None] <= s_of[part % T][:, None], 0.0, MASKED).astype(f32))
    b2 = rows(a["L0_ffn_b2"].reshape(-1))

    nc = bacc.Bacc("TRN2", target_bir_lowering=False, num_devices=1)
    arrays = {"x_t": x, "wtok_t": wtok, "setup": setup, "keep": keep, "w1": a["L0_ffn_W1"], "w2": a["L0_ffn_W2"],
              "b2_rows": np.ascontiguousarray(b2)}
    aps = [nc.dram_tensor(n, v.shape, mybir.dt.from_np(v.dtype), kind="ExternalInput").ap() for n, v in arrays.items()]
    out = nc.dram_tensor("out", (IMGS, T, D), F32, kind="ExternalOutput").ap()
    h2s = nc.dram_tensor("h2_rows", (TOK, D), F32, kind="Internal").ap()
    ws = nc.dram_tensor("mix_rows", (TOK, 4), F32, kind="Internal").ap()
    build(nc, *aps, out, h2s, ws)
    r = run_bass_kernel_spmd(nc, [arrays], core_ids=[0])
    return r.results[0]["out"]
```

```python
from contextlib import ExitStack

import numpy as np
import concourse.bass as bass
from concourse import mybir

F32 = mybir.dt.float32
F32R = mybir.dt.float32r
BF16 = mybir.dt.bfloat16
FP16 = mybir.dt.float16
ALU = mybir.AluOpType
ACT = mybir.ActivationFunctionType
AXX = mybir.AxisListType.X

P = 128
D = 256
NC_ = D // P
H, HD = 16, 16
HC = P // HD
T = 16
IMGS = 64
TOK = IMGS * T
GROUPS = TOK // P
GI = P // T
HALF_GROUPS = GROUPS // 2
HT = TOK // 2
KF = 768 // P
E = 4
FF = 1024
FC = FF // P
LN_EPS = 1e-5
RMS_EPS = 1.1920929e-07
SCALE = HD ** -0.5
MASKED = -1e30
LN3 = float(np.log(3.0))
PARTS = [(0, 0), (0, 1), (0, 2), (1, 0), (1, 1)]
THRESH = [None, -LN3, 0.0, LN3]
XR = 2
HR = 3
LOADS = [0, 1, 2, 3, 0]
UNITS = [(0, (0, 1), 0), (1, (0, 1), 1), (0, (2, 3), 0), (1, (2, 3), 1), (2, (0, 1, 2, 3), 2),
         (1, (4, 5, 6, 7), 1), (2, (4, 5, 6, 7), 2), (3, (0, 1, 2, 3), 3), (3, (4, 5, 6, 7), 3), (0, (4, 5, 6, 7), 4)]
LAST = len(UNITS) - 1
UNIT_BANKS = [len(groups) // (1 if n == LAST else 2) for n, (_, groups, _) in enumerate(UNITS)]
AHEAD_FROM = 0
EARLY_WORK = 4
BESIDE = 12
ACT_BLOCKS = 2
STAGES = 8


START = [{3: 2, 0: 0, 1: 0, 2: 1}, {7: 7, 6: 6, 5: 0, 4: -1}]
SPLIT_FROM = 0


def attention_slots(start):
    return [[(slot - at, g) for g, at in start.items() if 0 <= slot - at < STAGES]
            for slot in range(max(start.values()) + STAGES)]


PATCH_FROM = 20
PATCH_STEP = 2
FIRST, SECOND = attention_slots(START[0]), attention_slots(START[1])
_ffn = [(kind, n, fc) for n in range(len(UNITS)) for kind in ("layer1", "layer2") for fc in range(FC)]
_first = [("att", s, g) for slot in FIRST for s, g in slot]
for _i in range(HALF_GROUPS):
    _first.insert(PATCH_FROM + _i * (PATCH_STEP + 1), ("patch", 0, HALF_GROUPS + _i))
_done = _first.index(("att", STAGES - 1, 1)) + 1
_taken = [0, 0]


def ffn_items(work):
    items = []
    while _taken[0] < len(_ffn) and _taken[1] < work and all(
            ("att", STAGES - 1, g) in ORDER for g in UNITS[_ffn[_taken[0]][1]][1]):
        items.append(_ffn[_taken[0]])
        _taken[0] += 1
        _taken[1] += len(UNITS[items[-1][1]][1])
    return items


ORDER = _first[:_done]
_work = 0
_ahead = [("att", 0, 4), ("att", 0, 5), ("att", 1, 4), ("att", 1, 5)]
for _i, _item in enumerate(_first[_done:]):
    _work += EARLY_WORK
    ORDER += ffn_items(_work) + [_item]
    if _i >= AHEAD_FROM:
        ORDER += _ahead[_i - AHEAD_FROM:_i - AHEAD_FROM + 1]
for _slot in SECOND:
    _a = [("att", s, g) for s, g in _slot if ("att", s, g) not in ORDER]
    _parts = max(len(_a), 3)
    for _i in range(_parts):
        _work += BESIDE / _parts
        ORDER += _a[_i:_i + 1] + ffn_items(_work)
ORDER += ffn_items(1e9)
SPLIT = {SPLIT_FROM + i: (i // 4, i % 4) for i in range(16)}
for _m, _kind, _n, _fc in ((4, "layer1", 3, 0), (5, "layer2", 3, 0), (6, "layer2", 5, 0), (7, "layer2", 6, 0),
                           (8, "layer2", 6, 4), (9, "layer2", 7, 0)):
    for _q in range(4):
        SPLIT[ORDER.index((_kind, _n, _fc + _q))] = (_m, _q)

SETUP = {}
_at = 0
for _n, _w in (("wdq", 128), ("wuq", 128), ("wdkv", 256), ("wuk", 256), ("wkr", 128), ("wqr", 128),
               ("wuv", 256), ("wo", 128), ("wk", 256), ("bias", 256)):
    SETUP[_n] = (_at, _at + _w)
    _at += _w
SETUP_W = _at
KEEP = {}
_at = 0
for _n, _w in (("pos", 256), ("wq", 256), ("wu", 256), ("b1", 32), ("bu", 1), ("ident", 128),
               ("block", HC), ("causal", T), ("eps", 1), ("power", 1), ("mod", 4)):
    KEEP[_n] = (_at, _at + _w)
    _at += _w
KEEP_W = _at


def build(nc, x, wtok, setup, keep, w1, w2, b2, out):
    with ExitStack() as ctx:
        def sb(name, shape, dt=F32):
            return ctx.enter_context(nc.sbuf_tensor(name, shape, dt))

        def sem(name):
            return ctx.enter_context(nc.semaphore(name))

        keep_sb = sb("keep_sb", [P, KEEP_W])
        raw = sb("raw", [P, 2048])
        xt = sb("xt", [P, XR, KF, P])
        wtok_sb = sb("wtok_sb", [P, KF, D])
        wbd = sb("wbd", [P, 4, P])
        b2_sb = sb("b2_sb", [P, E, D])
        w1h = [sb(f"w1h{i}", [P, NC_, FF], F32R) for i in range(2)]
        w1l = [sb(f"w1l{i}", [P, NC_, FF], F32R) for i in range(2)]
        w2h = [sb(f"w2h{i}", [P, FC, D], F32R) for i in range(2)]
        w2l = [sb(f"w2l{i}", [P, FC, D], F32R) for i in range(2)]
        hid_h = sb("hid_h", [P, FC, HT], F32R)
        hid_l = sb("hid_l", [P, FC, HT], F32R)
        hid = sb("hid", [P, HR, HT])
        x2t_h = sb("x2t_h", [P, NC_, TOK], F32R)
        x2t_l = sb("x2t_l", [P, NC_, TOK], F32R)
        acc = sb("acc", [P, GROUPS, D])
        nk = sb("nk", [P, 4, 2, D])
        normed, kbuf = nk[:, :, 0, :], nk[:, :, 1, :]
        tbuf = sb("tbuf", [P, 4, 2, P])
        u_sb = tbuf[:, 3, :, :]
        wqk = keep_sb[:, KEEP["wq"][0]:KEEP["wq"][1]]
        sp16 = sb("sp16", [P, 4, 2, 2, P], FP16)
        kt3 = sb("kt3", [P, 4, 3, 2, P], BF16)
        v3 = sb("v3", [P, 4, 3, H, HD + 1], BF16)
        bd = sb("bd", [P, 2, 4, HC, P], FP16)
        bnst = sb("bnst", [P, 4, 6])
        mv = sb("mv", [P, 2 * GROUPS, 2])
        rstd = sb("rstd", [P, 2 * GROUPS])
        ssq = sb("ssq", [P, 4, 2 * H])
        rinv = sb("rinv", [P, 4, 2 * H])
        mx = sb("mx", [P, 4, 2 * GI])
        rsum = sb("rsum", [P, 4, H])
        zr = sb("zr", [P, GROUPS])
        zt = sb("zt", [P, GROUPS])
        ez = sb("ez", [P, GROUPS])
        uu = sb("uu", [P, GROUPS])
        wterm = sb("wterm", [P, GROUPS, 8])
        wmix = sb("wmix", [P, GROUPS, E])

        def kp(name):
            a, b = KEEP[name]
            return keep_sb[:, a:b]

        def setup_columns(a, b, rows=P):
            if b <= 1024:
                return acc[0:rows, GROUPS // 2:, :].rearrange("p a b -> p (a b)")[:, a:b]
            return hid[0:rows, 0:2, :].rearrange("p a b -> p (a b)")[:, a - 1024:b - 1024]

        def st(name, rows=P):
            return setup_columns(*SETUP[name], rows)

        psum = ctx.enter_context(nc.psum_tensor("psum", [P, 8, 512], F32))
        bank = [psum[:, i, :] for i in range(8)]

        def pair(g):
            return 2 * g if g < HALF_GROUPS else 2 * (g % 2)

        def patch_bank(g):
            return early(g) if g < HALF_GROUPS else bank[g]

        def early(g):
            return bank[pair(g)] if g < 6 else bank[pair(g) + 1]

        def after(g):
            return bank[(0, 2, 1, 3, 0, 2, 0, 2)[g]]

        def proj_banks(g):
            return psum[:, pair(g):pair(g) + 2, :]

        ld_keep, ld_setup, ld_bias, ld_b2 = sem("ld_keep"), sem("ld_setup"), sem("ld_bias"), sem("ld_b2")
        ld_wtok = [sem(f"ld_wtok{i}") for i in range(2)]
        ld_x = [sem(f"ld_x{i}") for i in range(XR)]
        ld_raw = [sem(f"ld_raw{i}") for i in range(4)]
        st_out = sem("st_out")
        setup_pe, setup_u, setup_done, ones_ready = sem("setup_pe"), sem("setup_u"), sem("setup_done"), sem("ones_ready")
        patch_done, hnt_done, proj_done, qkt_done = sem("patch_done"), sem("hnt_done"), sem("proj_done"), sem("qkt_done")
        score_done, pt_done, ctx_done, x2t_done = sem("score_done"), sem("pt_done"), sem("ctx_done"), sem("x2t_done")
        stats_ready, std_ready, hn_ready, hnt_ready = sem("stats_ready"), sem("std_ready"), sem("hn_ready"), sem("hnt_ready")
        sq_ready, va_ready, vrest_ready, v_ready = sem("sq_ready"), sem("va_ready"), sem("vrest_ready"), sem("v_ready")
        ssq_ready, rms_ready, qk_ready = sem("ssq_ready"), sem("rms_ready"), sem("qk_ready")
        kn_ready = sem("kn_ready")
        qka_ready, krest_ready, k_ready = sem("qka_ready"), sem("krest_ready"), sem("k_ready")
        qlo_ready, qbdv_ready, qbda_ready = sem("qlo_ready"), sem("qbdv_ready"), sem("qbda_ready")
        plo_ready, pbdv_ready, pbda_ready = sem("plo_ready"), sem("pbdv_ready"), sem("pbda_ready")
        s_ready, p_ready, pta_ready = sem("s_ready"), sem("p_ready"), sem("pta_ready")
        stats2_ready, std2_ready, x2_ready = sem("stats2_ready"), sem("std2_ready"), sem("x2_ready")
        x2th_ready, x2tl_ready = sem("x2th_ready"), sem("x2tl_ready")
        z_ready, ez_ready = sem("z_ready"), sem("ez_ready")
        wh_ready, wl_ready = sem("wh_ready"), sem("wl_ready")
        l1_done, hid_ready, hidl_ready = sem("l1_done"), sem("hid_ready"), sem("hidl_ready")
        l2_done, acc_ready = sem("l2_done"), sem("acc_ready")
        residual_ready = sem("residual_ready")
        bias_ready = sem("bias_ready")
        dve_chain, pool_chain = sem("dve_chain"), sem("pool_chain")

        def wslots(m):
            s = (m // 2) % 2
            hi, lo = ((w2h, w2l) if m % 2 else (w1h, w1l))
            return (hi[s][:, :, :].rearrange("p a b -> p (a b)"), lo[s][:, :, :].rearrange("p a b -> p (a b)"))

        def wait_slot_free(eng, m):
            if m // 2 >= 2:
                n = max(i for i, unit in enumerate(UNITS) if unit[2] == m // 2 - 2)
                if m % 2 == 0:
                    eng.wait_ge(l1_done, FC * (n + 1))
                else:
                    eng.wait_ge(l2_done, banks_before(n + 1))

        all_banks_from = FC * min(n for n in range(len(UNITS)) if GROUPS - 1 in UNITS[n][1])

        def hidden_bank(k):
            return bank[4 + k % 2] if k < all_banks_from else bank[(k - all_banks_from) % 6]

        def banks_before(n):
            return sum(UNIT_BANKS[:n])

        def l2_bank(n, j):
            return j if n == LAST else j // 2

        def l2_sums(n, j):
            i = l2_bank(n, j)
            b = bank[6 + i] if i < 2 else bank[i - 2]
            return b[:, 0:D] if n == LAST else b[:, (j % 2) * D:(j % 2 + 1) * D]

        def tokens(n):
            groups = UNITS[n][1]
            return slice(groups[0] * P, (groups[-1] + 1) * P), len(groups) * P

        bd_uses = [(s, g) for _, s, g in [i for i in ORDER if i[0] == "att"] if s in (3, 5)]

        def bd_slot(s, g):
            return bd_uses.index((s, g)) % 2

        def bd_block(s, g, i):
            return (bd[:, bd_slot(s, g), :, :, i * T:(i + 1) * T],
                    sp16[:, g % 4, :, :, :].rearrange("p s c (a q) -> p (s c) a q", q=T), kp("block")[:, i:i + 1])

        def wait_bd_free(eng, s, g):
            k = bd_uses.index((s, g)) - 2
            if k >= 0:
                s0, g0 = bd_uses[k]
                eng.wait_ge(score_done if s0 == 3 else ctx_done, g0 + 1)

        block = ctx.enter_context(nc.Block())

        @block.sync
        def _(sp):
            def load_x(g):
                if g >= XR:
                    sp.wait_ge(patch_done, g - XR + 1)
                sp.dma_start(xt[:, g % XR, :, :], x[g]).then_inc(ld_x[g % XR], 16)

            def load_raw(m):
                e = LOADS[m // 2]
                for q in range(4):
                    if m:
                        sp.wait_ge(wl_ready, 4 * (m - 1) + q + 1)
                    dst = raw[:, q * 512:(q + 1) * 512]
                    if m % 2 == 0:
                        c, f = q // 2, (q % 2) * 512
                        sp.dma_start(dst, w1[e][c * P:(c + 1) * P, f:f + 512]).then_inc(ld_raw[q], 16)
                    else:
                        sp.dma_start(dst.rearrange("p (c f) -> p c f", c=2),
                                     w2[e][2 * q * P:2 * (q + 1) * P, :].rearrange("(c p) f -> p c f", p=P)
                                     ).then_inc(ld_raw[q], 16)

            load_x(0)
            sp.dma_start(wtok_sb[:, 0:KF // 2, :], wtok[:, 0:KF // 2, :]).then_inc(ld_wtok[0], 16)
            sp.dma_start(wtok_sb[:, KF // 2:, :], wtok[:, KF // 2:, :]).then_inc(ld_wtok[1], 16)
            sp.dma_start(keep_sb[:, :], keep).then_inc(ld_keep, 16)
            for a, b, loaded in ((*SETUP["bias"], ld_bias), (0, 1024, ld_setup), (1024, SETUP["bias"][0], ld_setup)):
                sp.dma_start(setup_columns(a, b), setup[:, a:b]).then_inc(loaded, 16)
            load_x(1)
            load_raw(0)
            load_x(2)
            load_x(3)
            load_raw(1)
            load_x(4)
            load_x(5)
            load_raw(2)
            load_raw(3)
            load_x(6)
            load_x(7)
            sp.dma_start(b2_sb[:, :, :].rearrange("p e d -> p (e d)"), b2).then_inc(ld_b2, 16)
            for m in range(4, 2 * len(LOADS)):
                load_raw(m)
            for n, (_, groups, _) in enumerate(UNITS):
                for g in groups:
                    if all(g not in later for _, later, _ in UNITS[n + 1:]):
                        sp.wait_ge(acc_ready, banks_before(n) + l2_bank(n, groups.index(g)) + 1)
                        sp.dma_start(out[g * GI:(g + 1) * GI].rearrange("b s d -> (b s) d"),
                                     acc[:, g, :]).then_inc(st_out, 16)
            sp.wait_ge(st_out, 16 * GROUPS)

        @block.tensor
        def _(pe):
            ident = kp("ident")

            def mm(o, a, b, first, last, group=True):
                return pe.matmul(o, a, b, start=first, stop=last, skip_group_check=not group)

            def setup_products():
                pe.wait_ge(ld_keep, 16)
                pe.wait_ge(ld_setup, 32)
                for c in range(2):
                    r = mm(bank[5][:, c * P:(c + 1) * P], st("wuv", HD)[:, c * P:(c + 1) * P], st("wo", HD), True, True)
                r.then_inc(setup_pe, 1)
                mm(bank[4][:, 0:P], st("wdq"), st("wuq"), True, True)
                for c in range(2):
                    mm(bank[4][:, P:2 * P], st("wdkv")[:, c * P:(c + 1) * P], st("wuk")[:, c * P:(c + 1) * P], c == 0, c == 1)
                mm(bank[4][:, 2 * P:3 * P], st("wkr", 64), st("wqr", 64), True, True)

            def setup_v():
                pe.wait_ge(setup_u, 1)
                for c in range(2):
                    r = mm(bank[4][:, 3 * P:4 * P], st("wdkv")[:, c * P:(c + 1) * P], u_sb[:, c, :], c == 0, c == 1)
                r.then_inc(setup_pe, 1)

            def step(s, g):
                gg = g % 4
                if s == 0:
                    pe.wait_ge(ld_x[g % XR], 16 * (g // XR + 1))
                    if g == 2:
                        pe.wait_ge(setup_done, 1)
                    elif g >= 4:
                        pe.wait_ge(qk_ready, 4)
                        pe.wait_ge(vrest_ready, 4)
                    for c in range(KF):
                        if g == 0 and c % (KF // 2) == 0:
                            pe.wait_ge(ld_wtok[c // (KF // 2)], 16)
                        r = mm(patch_bank(g)[:, 0:D], xt[:, g % XR, c, :], wtok_sb[:, c, :], c == 0, c == KF - 1)
                    r.then_inc(patch_done, 1)
                elif s == 1:
                    pe.wait_ge(hn_ready, g + 1)
                    if g in (4, 5):
                        pe.wait_ge(x2tl_ready, g - 3)
                    elif g >= 6:
                        pe.wait_ge(qk_ready, g - 1)
                        pe.wait_ge(vrest_ready, g - 1)
                    for c in range(NC_):
                        r = pe.transpose(early(g)[:, c * P:(c + 1) * P], normed[:, gg, c * P:(c + 1) * P], ident)
                    r.then_inc(hnt_done, 1)
                elif s == 2:
                    if g == 0:
                        pe.wait_ge(setup_done, 1)
                    pe.wait_ge(hnt_ready, g + 1)
                    if g >= 4:
                        pe.wait_ge(x2tl_ready, g - 1)
                    for c in range(NC_):
                        r = mm(proj_banks(g)[:, c, :], tbuf[:, gg, c, :],
                               wbd[:, :, :].rearrange("p a b -> p (a b)"), True, True)
                    r.then_inc(proj_done, 1)
                elif s == 3:
                    pe.wait_ge(qk_ready, g + 1)
                    pe.wait_ge(vrest_ready, g + 1)
                    for c in range(NC_):
                        pe.transpose(after(g)[:, c * P:(c + 1) * P], normed[:, gg, c * P:(c + 1) * P], ident)
                    for c in range(NC_):
                        r = pe.transpose(after(g)[:, (2 + c) * P:(3 + c) * P], kbuf[:, gg, c * P:(c + 1) * P], ident)
                    r.then_inc(qkt_done, 1)
                elif s == 4:
                    pe.wait_ge(qbdv_ready, g + 1)
                    pe.wait_ge(qbda_ready, g + 1)
                    pe.wait_ge(k_ready, g + 1)
                    for c in range(NC_):
                        for b in range(GI):
                            o = (c * GI + b) * T
                            for n, (a, m) in enumerate(PARTS):
                                r = mm(after(g)[:, o:o + T], bd[:, bd_slot(3, g), 2 * a + c, b, :],
                                       kt3[:, gg, m, c, b * T:(b + 1) * T], n == 0, n == len(PARTS) - 1)
                    r.then_inc(score_done, 1)
                elif s == 5:
                    pe.wait_ge(p_ready, g + 1)
                    for c in range(NC_):
                        r = pe.transpose(after(g)[:, c * P:(c + 1) * P], kbuf[:, gg, c * P:(c + 1) * P], ident)
                    r.then_inc(pt_done, 1)
                elif s == 6:
                    pe.wait_ge(pbdv_ready, g + 1)
                    pe.wait_ge(pbda_ready, g + 1)
                    pe.wait_ge(v_ready, g + 1)
                    for h in range(H):
                        c, hc = h // HC, h % HC
                        for n, (a, m) in enumerate(PARTS):
                            r = mm(after(g)[:, h * (HD + 1):(h + 1) * (HD + 1)], bd[:, bd_slot(5, g), 2 * a + c, hc, :],
                                   v3[:, gg, m, h, :], n == 0, n == len(PARTS) - 1)
                    r.then_inc(ctx_done, 1)
                else:
                    pe.wait_ge(x2_ready, g + 1)
                    for c in range(NC_):
                        r = pe.transpose(after(g)[:, c * P:(c + 1) * P], normed[:, gg, c * P:(c + 1) * P], ident)
                    r.then_inc(x2t_done, 1)

            def layer1(n, fc):
                _, groups, load = UNITS[n]
                t, width = tokens(n)
                k = n * FC + fc
                if fc == 0:
                    pe.wait_ge(wl_ready, 4 * (2 * load + 1))
                    pe.wait_ge(x2tl_ready, groups[-1] + 1)
                    if n == 0:
                        pe.wait_ge(residual_ready, HALF_GROUPS)
                since = k - all_banks_from
                if k >= 2 and since < 0:
                    pe.wait_ge(hid_ready, k - 1)
                elif since >= 4:
                    pe.wait_ge(hid_ready, k - 5 if since >= 6 else all_banks_from)
                f = slice(fc * P, (fc + 1) * P)
                ps = hidden_bank(k)[:, 0:width]
                for c in range(NC_):
                    mm(ps, w1h[load % 2][:, c, f], x2t_h[:, c, t], c == 0, False)
                    mm(ps, w1h[load % 2][:, c, f], x2t_l[:, c, t], False, False)
                    r = mm(ps, w1l[load % 2][:, c, f], x2t_h[:, c, t], False, c == NC_ - 1)
                r.then_inc(l1_done, 1)

            def layer2(n, fc):
                _, groups, load = UNITS[n]
                if fc == 0:
                    pe.wait_ge(wl_ready, 4 * (2 * load + 2))
                    if n:
                        pe.wait_ge(acc_ready, banks_before(n))
                if n == LAST:
                    j = fc // 2
                    if fc == 4:
                        pe.wait_ge(hid_ready, (n + 1) * FC)
                    todo = [(j, f) for f in range((fc % 2) * FC // 2, (fc % 2 + 1) * FC // 2)]
                else:
                    pe.wait_ge(hidl_ready, n * FC + fc + 1)
                    todo = [(j, fc) for j in range(len(groups))]
                for j, f in todo:
                    if n == LAST and j == 0:
                        pe.wait_ge(hidl_ready, n * FC + f + 1)
                    t = slice(j * P, (j + 1) * P)
                    o = l2_sums(n, j)
                    mm(o, hid_h[:, f, t], w2h[load % 2][:, f, :], f == 0 and (j % 2 == 0 or n == LAST), False, False)
                    mm(o, hid_h[:, f, t], w2l[load % 2][:, f, :], False, False, False)
                    r = mm(o, hid_l[:, f, t], w2h[load % 2][:, f, :], False, f == FC - 1, False)
                    if f == FC - 1 and (j % 2 or n == LAST):
                        r.then_inc(l2_done, 1)

            for at, (kind, a, b) in enumerate(ORDER):
                if (kind, a) != ("att", 0) or b < HALF_GROUPS:
                    {"att": step, "patch": step, "layer1": layer1, "layer2": layer2}[kind](a, b)
                if at == 0:
                    setup_products()
                elif at == 1:
                    setup_v()

        @block.scalar
        def _(act):
            def two(ap):
                return ap.rearrange("p (a b) -> p a b", a=2)

            def step(s, g):
                gg = g % 4
                if s == 1:
                    act.wait_ge(hnt_done, g + 1)
                    act.activation(tbuf[:, gg, :, :], two(early(g)[:, 0:D]), ACT.Copy).then_inc(hnt_ready, 1)
                elif s == 2:
                    act.wait_ge(proj_done, g + 1)
                    ps = proj_banks(g)
                    act.activation(nk[:, gg, :, :].rearrange("p a (c f) -> p c a f", c=NC_),
                                   ps[:, :, 0:2 * P].rearrange("p c (a f) -> p c a f", a=2),
                                   ACT.Square).then_inc(sq_ready, 1)
                    if g == 0:
                        act.wait_ge(ones_ready, 1)
                    act.activation(v3[:, gg, 0, :, 0:HD].rearrange("p (c h) d -> p c h d", c=NC_),
                                   ps[:, :, 3 * P:4 * P].rearrange("p c (h d) -> p c h d", h=HC),
                                   ACT.Copy).then_inc(va_ready, 1)
                elif s == 3:
                    act.wait_ge(qkt_done, g + 1)
                    act.activation(sp16[:, gg, 0, :, :], two(after(g)[:, 0:D]), ACT.Copy)
                    act.activation(kt3[:, gg, 0, :, :], two(after(g)[:, D:2 * D]), ACT.Copy).then_inc(qka_ready, 1)
                elif s == 5:
                    act.wait_ge(pt_done, g + 1)
                    act.activation(sp16[:, gg, 0, :, :], two(after(g)[:, 0:D]), ACT.Copy).then_inc(pta_ready, 1)
                elif s == 7:
                    act.wait_ge(x2t_done, g + 1)
                    act.activation(x2t_h[:, :, g * P:(g + 1) * P], two(after(g)[:, 0:D]), ACT.Copy).then_inc(x2th_ready, 1)

            def spread(s, g):
                wait_bd_free(act, s, g)
                for i in range(ACT_BLOCKS):
                    o, a, m = bd_block(s, g, i)
                    r = act.activation(o, a, ACT.Copy, scale=m)
                return r

            def finish(s, g):
                gg = g % 4
                if s == 2:
                    act.wait_ge(ssq_ready, g + 1)
                    if g == 0:
                        act.wait_ge(ld_keep, 16)
                    act.activation(rinv[:, gg, :], ssq[:, gg, :], ACT.Sqrt, bias=kp("eps")).then_inc(rms_ready, 1)
                elif s == 3:
                    act.wait_ge(qlo_ready, g + 1)
                    spread(s, g).then_inc(qbda_ready, 1)
                elif s == 4:
                    act.wait_ge(s_ready, g + 1)
                    act.activation(kbuf[:, gg, :], kbuf[:, gg, :], ACT.Exp).then_inc(p_ready, 1)
                elif s == 5:
                    act.wait_ge(plo_ready, g + 1)
                    spread(s, g).then_inc(pbda_ready, 1)

            def routing(r):
                gs = slice(2 * r, 2 * r + 2)
                act.wait_ge(z_ready, r + 1)
                act.activation(ez[:, gs], zt[:, gs], ACT.Exp, scale=-1.0).then_inc(ez_ready, 1)

            def split_hi(m, quarter):
                act.wait_ge(ld_raw[quarter], 16 * (m + 1))
                wait_slot_free(act, m)
                f = slice(quarter * 512, (quarter + 1) * 512)
                act.activation(wslots(m)[0][:, f], raw[:, f], ACT.Copy).then_inc(wh_ready, 1)

            def hidden(n, fc):
                e, width = UNITS[n][0], tokens(n)[1]
                k = n * FC + fc
                act.wait_ge(l1_done, k + 1)
                if k >= HR:
                    act.wait_ge(hidl_ready, k - HR + 1)
                b1 = kp("b1")[:, e * FC + fc:e * FC + fc + 1]
                ps = hidden_bank(k)[:, 0:width]
                act.activation(hid_h[:, fc, 0:width], ps, ACT.Relu, bias=b1)
                act.activation(hid[:, k % HR, 0:width], ps, ACT.Relu, bias=b1).then_inc(hid_ready, 1)

            held = None
            for at, (kind, a, b) in enumerate(ORDER):
                if held and kind == "att" and held[1] == b:
                    finish(*held)
                    held = None
                if kind == "att":
                    step(a, b)
                elif kind == "layer1":
                    hidden(a, b)
                if held:
                    finish(*held)
                    held = None
                if kind == "att" and a in (2, 3, 4, 5):
                    held = (a, b)
                if at in SPLIT:
                    split_hi(*SPLIT[at])
                if kind == "att" and a == STAGES - 1 and b % 2:
                    routing(b // 2)

        @block.gpsimd
        def _(pool):
            chained = [0]

            def link(ins):
                chained[0] += 1
                ins.then_inc(pool_chain, 1)
                pool.wait_ge(pool_chain, chained[0])

            def step(s, g):
                gg = g % 4
                if s == 0:
                    if g == 0:
                        pool.wait_ge(ld_keep, 16)
                    pool.wait_ge(stats_ready, g + 1)
                    rsqrt(g, std_ready)
                elif s == 6:
                    pool.wait_ge(stats2_ready, g + 1)
                    rsqrt(GROUPS + g, std2_ready)
                elif s == 2:
                    pool.wait_ge(vrest_ready, g + 1)
                    rest = tbuf[:, gg, :, :].rearrange("p c (h d) -> p (c h) d", d=HD)
                    link(pool.tensor_copy(v3[:, gg, 1, :, 0:HD], rest))
                    pool.tensor_tensor(v3[:, gg, 2, :, 0:HD], rest, v3[:, gg, 1, :, 0:HD], ALU.subtract).then_inc(v_ready, 1)
                elif s == 3:
                    pool.wait_ge(krest_ready, g + 1)
                    rest = kbuf[:, gg, :].rearrange("p (c t) -> p c t", c=NC_)
                    link(pool.tensor_copy(kt3[:, gg, 1, :, :], rest))
                    pool.tensor_tensor(kt3[:, gg, 2, :, :], rest, kt3[:, gg, 1, :, :], ALU.subtract).then_inc(k_ready, 1)

            def rsqrt(at, ready):
                r = rstd[:, at:at + 1]
                pool.tensor_tensor(r, r, kp("power"), ALU.pow).then_inc(ready, 1)

            def split_lo(m, quarter):
                pool.wait_ge(wh_ready, 4 * m + quarter + 1)
                hi, lo = wslots(m)
                f = slice(quarter * 512, (quarter + 1) * 512)
                pool.tensor_tensor(lo[:, f], raw[:, f], hi[:, f].bitcast(F32), ALU.subtract).then_inc(wl_ready, 1)

            link(pool.memset(v3[:, :, :, :, :].rearrange("p a b h d -> p (a b h d)"), 0.0))
            pool.memset(v3[:, :, 0, :, HD:HD + 1], 1.0).then_inc(ones_ready, 1)
            for at, (kind, a, b) in enumerate(ORDER):
                if kind == "att":
                    step(a, b)
                if at in SPLIT:
                    split_lo(*SPLIT[at])

        @block.vector
        def _(dve):
            chained = [0]

            def link(ins):
                chained[0] += 1
                ins.then_inc(dve_chain, 1)
                dve.wait_ge(dve_chain, chained[0])

            def setup_position():
                dve.wait_ge(ld_keep, 16)
                dve.wait_ge(ld_bias, 16)
                link(dve.tensor_tensor(kp("pos"), kp("pos"), st("bias"), ALU.add))

            def setup_values():
                dve.wait_ge(setup_pe, 1)
                dve.tensor_copy(u_sb, bank[5][:, 0:2 * P].rearrange("p (a b) -> p a b", a=2)).then_inc(setup_u, 1)

            def setup_weights():
                dve.wait_ge(setup_pe, 2)
                link(dve.tensor_tensor(wbd[:, :, :].rearrange("p n (h d) -> p n h d", h=HC),
                                       bank[4][:, :].rearrange("p (n h d) -> p n h d", n=4, h=HC),
                                       kp("block").unsqueeze(1).unsqueeze(3).to_broadcast([P, 4, HC, HD]), ALU.mult))
                link(dve.scalar_tensor_tensor(wbd[:, 2, :], wbd[:, 2, :], HD ** 0.5 * SCALE, kp("wq")[:, 0:P],
                                              ALU.mult, ALU.mult))
                dve.scalar_tensor_tensor(wqk, kp("wq"), HD * SCALE, st("wk"), ALU.mult, ALU.mult).then_inc(setup_done, 1)

            def residual(g):
                dve.wait_ge(patch_done, g + 1)
                return dve.tensor_tensor(acc[:, g, :], patch_bank(g)[:, 0:D], kp("pos"), ALU.add)

            def stats(g, at):
                link(dve.bn_stats(bnst[:, g % 4, :], acc[:, g, :]))
                link(dve.bn_aggr(mv[:, at, :], bnst[:, g % 4, :]))
                return dve.tensor_scalar(rstd[:, at:at + 1], mv[:, at, 1:2], LN_EPS, None, ALU.add)

            def normalise(g, at, std, ready):
                gg = g % 4
                dve.wait_ge(std, g + 1)
                dve.tensor_scalar(normed[:, gg, :], acc[:, g, :], mv[:, at, 0:1], rstd[:, at:at + 1],
                                  ALU.subtract, ALU.mult).then_inc(ready, 1)

            def spread(s, g):
                for i in range(ACT_BLOCKS, HC):
                    o, a, m = bd_block(s, g, i)
                    r = dve.tensor_scalar(o, a, m, None, ALU.mult)
                return r

            def heads(ap):
                return ap.rearrange("p (h d) -> p h d", d=HD)

            def chunked_heads(ap):
                return ap.rearrange("p c (h d) -> p c h d", d=HD)

            def norm_qk(g):
                gg = g % 4
                ps = proj_banks(g)
                dve.wait_ge(rms_ready, g + 1)
                link(dve.reciprocal(rinv[:, gg, :], rinv[:, gg, :]))
                rb = rinv[:, gg, :].rearrange("p (a c h) -> p c a h", c=NC_, a=2).unsqueeze(4).to_broadcast(
                    [P, NC_, 2, HC, HD])
                qn = normed[:, gg, :].rearrange("p (c h d) -> p c h d", c=NC_, d=HD)
                kn = kbuf[:, gg, :].rearrange("p (c h d) -> p c h d", c=NC_, d=HD)
                kn2 = kbuf[:, gg, :].rearrange("p (c f) -> p c f", c=NC_)
                dve.tensor_tensor(kn, chunked_heads(ps[:, :, P:2 * P]), rb[:, :, 1], ALU.mult).then_inc(kn_ready, 1)
                dve.tensor_tensor(qn, chunked_heads(ps[:, :, 0:P]), rb[:, :, 0], ALU.mult)
                dve.wait_ge(kn_ready, g + 1)
                link(dve.tensor_tensor(kbuf[:, gg, :], kbuf[:, gg, :], wqk, ALU.mult))
                dve.tensor_tensor(kn2, kn2, ps[:, :, 2 * P:3 * P], ALU.add).then_inc(qk_ready, 1)

            def step(s, g):
                gg = g % 4
                if s == 0:
                    if g < HALF_GROUPS:
                        link(residual(g))
                    else:
                        dve.wait_ge(residual_ready, g - HALF_GROUPS + 1)
                    stats(g, g).then_inc(stats_ready, 1)
                elif s == 2:
                    dve.wait_ge(sq_ready, g + 1)
                    dve.tensor_reduce(ssq[:, gg, :], nk[:, gg, :, :].rearrange("p a (h d) -> p (a h) d", d=HD),
                                      AXX, ALU.add).then_inc(ssq_ready, 1)
                    dve.wait_ge(va_ready, g + 1)
                    dve.tensor_tensor(chunked_heads(tbuf[:, gg, :, :]), chunked_heads(proj_banks(g)[:, :, 3 * P:4 * P]),
                                      v3[:, gg, 0, :, 0:HD].rearrange("p (c h) d -> p c h d", c=NC_),
                                      ALU.subtract).then_inc(vrest_ready, 1)
                elif s == 3:
                    dve.wait_ge(qka_ready, g + 1)
                    b2v = after(g)[:, :].rearrange("p (n c t) -> p n c t", n=2, c=NC_)
                    dve.tensor_tensor(kbuf[:, gg, :].rearrange("p (c t) -> p c t", c=NC_), b2v[:, 1], kt3[:, gg, 0, :, :],
                                      ALU.subtract).then_inc(krest_ready, 1)
                    dve.tensor_tensor(sp16[:, gg, 1, :, :], b2v[:, 0], sp16[:, gg, 0, :, :],
                                      ALU.subtract).then_inc(qlo_ready, 1)
                    wait_bd_free(dve, s, g)
                    dve.wait_ge(qlo_ready, g + 1)
                    spread(s, g).then_inc(qbdv_ready, 1)
                elif s == 4:
                    dve.wait_ge(score_done, g + 1)
                    sc = kbuf[:, gg, :].rearrange("p (a k) -> p a k", k=T)
                    link(dve.tensor_tensor(sc, after(g)[:, 0:D].rearrange("p (a k) -> p a k", k=T),
                                           kp("causal").unsqueeze(1).to_broadcast([P, 2 * GI, T]), ALU.add))
                    link(dve.tensor_reduce(mx[:, gg, :], sc, AXX, ALU.max))
                    dve.tensor_tensor(sc, sc, mx[:, gg, :].unsqueeze(2).to_broadcast([P, 2 * GI, T]),
                                      ALU.subtract).then_inc(s_ready, 1)
                elif s == 5:
                    dve.wait_ge(pta_ready, g + 1)
                    dve.tensor_tensor(sp16[:, gg, 1, :, :], after(g)[:, 0:D].rearrange("p (c t) -> p c t", c=NC_),
                                      sp16[:, gg, 0, :, :], ALU.subtract).then_inc(plo_ready, 1)
                    wait_bd_free(dve, s, g)
                    dve.wait_ge(plo_ready, g + 1)
                    spread(s, g).then_inc(pbdv_ready, 1)
                elif s == 6:
                    dve.wait_ge(ctx_done, g + 1)
                    cx = after(g)[:, 0:H * (HD + 1)].rearrange("p (h d) -> p h d", d=HD + 1)
                    link(dve.reciprocal(rsum[:, gg, :], cx[:, :, HD]))
                    link(dve.tensor_tensor(heads(kbuf[:, gg, :]), cx[:, :, 0:HD],
                                           rsum[:, gg, :].unsqueeze(2).to_broadcast([P, H, HD]), ALU.mult))
                    link(dve.tensor_tensor(acc[:, g, :], acc[:, g, :], kbuf[:, gg, :], ALU.add))
                    at = GROUPS + g
                    stats(g, at).then_inc(stats2_ready, 1)
                    dve.scalar_tensor_tensor(kbuf[:, gg, :], acc[:, g, :], mv[:, at, 0:1], kp("wu"),
                                             ALU.subtract, ALU.mult, accum_out=zr[:, g:g + 1])
                elif s == 7:
                    dve.wait_ge(x2th_ready, g + 1)
                    cols = slice(g * P, (g + 1) * P)
                    dve.tensor_tensor(x2t_l[:, :, cols], after(g)[:, 0:D].rearrange("p (c t) -> p c t", c=NC_),
                                      x2t_h[:, :, cols].bitcast(F32), ALU.subtract).then_inc(x2tl_ready, 1)

            def finish(s, g):
                if s == 0:
                    normalise(g, g, std_ready, hn_ready)
                elif s == 2:
                    norm_qk(g)
                elif s == 6:
                    normalise(g, GROUPS + g, std2_ready, x2_ready)

            def routing(r):
                gs = slice(2 * r, 2 * r + 2)
                dve.wait_ge(x2_ready, 2 * (r + 1))
                link(dve.tensor_tensor(zt[:, gs], zr[:, gs], rstd[:, GROUPS + 2 * r:GROUPS + 2 * r + 2], ALU.mult))
                dve.tensor_scalar(zt[:, gs], zt[:, gs], kp("bu"), None, ALU.add).then_inc(z_ready, 1)
                dve.wait_ge(ez_ready, r + 1)
                link(dve.tensor_scalar(uu[:, gs], ez[:, gs], 1.0, None, ALU.add))
                link(dve.reciprocal(uu[:, gs], uu[:, gs]))
                for i in range(1, 4):
                    last = dve.tensor_scalar(wterm[:, gs, i], zt[:, gs], THRESH[i], 1.0 / (i + 1), ALU.is_gt, ALU.mult)
                link(last)
                for i in range(1, 4):
                    dve.tensor_tensor(wterm[:, gs, i], wterm[:, gs, i], uu[:, gs], ALU.mult)
                link(dve.tensor_copy(wterm[:, gs, 0], uu[:, gs]))
                link(dve.tensor_copy(wterm[:, gs, 4:8], wterm[:, gs, 0:4]))
                link(dve.tensor_scalar(wmix[:, gs, :], wterm[:, gs, 4:8], kp("mod")[:, 0:1], None, ALU.mult))
                for j in range(1, 4):
                    link(dve.scalar_tensor_tensor(wmix[:, gs, :], wterm[:, gs, 4 - j:8 - j], kp("mod")[:, j:j + 1],
                                                  wmix[:, gs, :], ALU.mult, ALU.add))

            def hidden_lo(n, fc):
                k, width = n * FC + fc, tokens(n)[1]
                dve.wait_ge(hid_ready, k + 1)
                dve.tensor_tensor(hid_l[:, fc, 0:width], hid[:, k % HR, 0:width], hid_h[:, fc, 0:width].bitcast(F32),
                                  ALU.subtract).then_inc(hidl_ready, 1)

            def mix_bias(n):
                e, groups, _ = UNITS[n]
                if n == 0:
                    dve.wait_ge(ld_b2, 16)
                else:
                    dve.wait_ge(acc_ready, banks_before(n))
                for g in groups:
                    r = dve.scalar_tensor_tensor(acc[:, g, :], b2_sb[:, e, :], wmix[:, g, e:e + 1], acc[:, g, :],
                                                 ALU.mult, ALU.add)
                r.then_inc(bias_ready, 1)

            def mix(n):
                e, groups, _ = UNITS[n]
                dve.wait_ge(bias_ready, n + 1)
                for j, g in enumerate(groups):
                    if j % 2 == 0 or n == LAST:
                        dve.wait_ge(l2_done, banks_before(n) + l2_bank(n, j) + 1)
                    r = dve.scalar_tensor_tensor(acc[:, g, :], l2_sums(n, j), wmix[:, g, e:e + 1], acc[:, g, :],
                                                 ALU.mult, ALU.add)
                    if j % 2 or n == LAST:
                        r.then_inc(acc_ready, 1)

            setup_position()
            held = None
            for at, (kind, a, b) in enumerate(ORDER):
                if held and kind == "att" and held[1] == b:
                    finish(*held)
                    held = None
                if kind == "att":
                    step(a, b)
                elif kind == "layer1":
                    if b == 0 and a:
                        mix(a - 1)
                    hidden_lo(a, b)
                elif kind == "layer2" and b == (0 if a == LAST else FC - 2):
                    mix_bias(a)
                if held:
                    finish(*held)
                    held = None
                if kind == "att":
                    if a in (0, 2, 6):
                        held = (a, b)
                    if a == STAGES - 1 and b % 2:
                        routing(b // 2)
                if kind == "patch":
                    residual(b).then_inc(residual_ready, 1)
                if at == 0:
                    setup_values()
                elif at == 1:
                    setup_weights()
            mix(len(UNITS) - 1)


def kernel(**inputs):
    import concourse.bacc as bacc
    from concourse.bass_utils import run_bass_kernel_spmd

    a = {k: np.ascontiguousarray(v) for k, v in inputs.items()}

    x = a["x"].reshape(GROUPS, GI, 3, 4, 16, 4, 16)
    x = x.transpose(0, 2, 4, 6, 1, 3, 5).reshape(GROUPS, KF, P, P)
    x = np.ascontiguousarray(x.transpose(0, 2, 1, 3))
    wtok = np.ascontiguousarray(a["L0_tok_W"].reshape(D, KF, P).transpose(2, 1, 0))
    at = {k[len("L0_attn_"):]: v for k, v in a.items() if k.startswith("L0_attn_")}

    def chunks(w):
        return w.reshape(2, P, -1).transpose(1, 0, 2).reshape(P, -1)

    def rows(v):
        return np.broadcast_to(v.reshape(1, -1), (P, v.size))

    f32 = np.float32
    setup = np.zeros((P, SETUP_W), f32)
    keep = np.zeros((P, KEEP_W), f32)

    def put(t, where, name, v):
        s = where[name][0]
        t[:v.shape[0], s:s + v.shape[1]] = v
    put(setup, SETUP, "wdq", np.tile(at["W_DQ"], (1, HC)))
    put(setup, SETUP, "wuq", np.tile(at["W_UQ"].T, (1, HC)))
    put(setup, SETUP, "wdkv", chunks(np.tile(at["W_DKV"], (1, HC))))
    put(setup, SETUP, "wuk", chunks(np.tile(at["W_UKV"][:HD].T, (1, HC))))
    put(setup, SETUP, "wkr", np.tile(at["W_KR"], (1, HC)))
    put(setup, SETUP, "wqr", np.tile(at["W_QR"], (1, HC)))
    put(setup, SETUP, "wuv", at["W_UKV"][HD:])
    put(setup, SETUP, "wo", np.tile(at["W_O"].T, (1, HC)))
    put(setup, SETUP, "wk", rows(np.tile(at["k_norm_w"], H)))
    put(setup, SETUP, "bias", rows(a["L0_tok_b"]))
    keep[:, KEEP["eps"][0]] = HD * RMS_EPS
    keep[:, KEEP["power"][0]] = -0.5
    put(keep, KEEP, "pos", np.tile(a["L0_tok_pos_emb"].reshape(T, D), (GI, 1)))
    put(keep, KEEP, "wq", rows(np.tile(at["q_norm_w"], H)))
    put(keep, KEEP, "wu", rows(a["L0_ffn_Wu"]))
    put(keep, KEEP, "b1", a["L0_ffn_b1"].reshape(E * FC, P).T)
    put(keep, KEEP, "bu", rows(a["L0_ffn_bu"]))
    part = np.arange(P)
    put(keep, KEEP, "ident", np.eye(P, dtype=f32))
    put(keep, KEEP, "mod", (part[:, None] % 4 == np.arange(4)[None]).astype(f32))
    put(keep, KEEP, "block", (part[:, None] // T == np.arange(HC)[None]).astype(f32))
    put(keep, KEEP, "causal", np.where(np.arange(T)[None] <= part[:, None] % T, 0.0, MASKED).astype(f32))
    b2 = rows(a["L0_ffn_b2"].reshape(-1))

    nc = bacc.Bacc("TRN2", target_bir_lowering=False, num_devices=1)
    arrays = {"x_t": x, "wtok_t": wtok, "setup": setup, "keep": keep, "w1": a["L0_ffn_W1"], "w2": a["L0_ffn_W2"],
              "b2_rows": np.ascontiguousarray(b2)}
    aps = [nc.dram_tensor(n, v.shape, mybir.dt.from_np(v.dtype), kind="ExternalInput").ap() for n, v in arrays.items()]
    out = nc.dram_tensor("out", (IMGS, T, D), F32, kind="ExternalOutput").ap()
    build(nc, *aps, out)
    r = run_bass_kernel_spmd(nc, [arrays], core_ids=[0])
    return r.results[0]["out"]
```
